# Optimizing a Trainium2 kernel written in Bass

```python
import numpy as np
import jax
import jax.numpy as jnp

def _softmax(x, axis=-1):
    return jax.nn.softmax(x, axis=axis)
def _gelu(x):
    return jax.nn.gelu(x, approximate=True)
def _silu(x):
    return jax.nn.silu(x)
def _sigmoid(x):
    return jax.nn.sigmoid(x)
def _layernorm(x, axis=-1, eps=1e-5):
    m = jnp.mean(x, axis=axis, keepdims=True)
    v = jnp.var(x, axis=axis, keepdims=True)
    return (x - m) / jnp.sqrt(v + eps)
def _scatter_add(tgt, idx, src, axis=0):
    return tgt.at[idx].add(src)
def _segment_sum(src, seg, n):
    return jax.ops.segment_sum(src, seg, n)

kernel_name = 'mk_conv_preact_d2_conv_nchw256_140a3e'

def setup_inputs(seed: int = 0):
    np.random.seed(seed)
    _w = jnp.asarray
    def _rec_inputs():
        import jax
        import jax.numpy as jnp
        _gk = jax.random.key(seed)
        x = -0.0006537 + 1.001 * jax.random.normal(jax.random.fold_in(_gk, 1), (1, 256, 96, 96), jnp.float32)
        return x
    x = _rec_inputs()
    def _L0_conv_setup():
        import jax, jax.numpy as jnp
        import numpy as np
        CUTOFF = 0.05

        def _freq_filter(x_chw, filter_type):
            x = jax.lax.stop_gradient(x_chw)
            C, H, W = x.shape
            a = jnp.abs(x)
            mn = a.min(axis=(1, 2), keepdims=True)
            ptp = a.max(axis=(1, 2), keepdims=True) - mn
            q = jnp.floor(255.0 * (a - mn) / ptp)
            f = jnp.fft.fftshift(jnp.fft.fft2(q), axes=(-2, -1))
            crow, ccol = (H // 2, W // 2)
            dr, dc = (int(CUTOFF * crow), int(CUTOFF * ccol))
            m = jnp.zeros((H, W), dtype=q.dtype)
            m = m.at[crow - dr:crow + dr, ccol - dc:ccol + dc].set(1.0)
            if filter_type == 'low_pass':
                m = 1.0 - m
            out = jnp.abs(jnp.fft.ifft2(jnp.fft.ifftshift(f * m, axes=(-2, -1))))
            return out.astype(x_chw.dtype)

        def _conv1x1(x, w, b):
            return jnp.einsum('oc,bchw->bohw', w, x) + b[None, :, None, None]
        key = jax.random.key(seed)
        ks = jax.random.split(key, 7)
        B, C, H, W = (1, 256, 96, 96)
        fuse = jax.random.normal(ks[0], (B, C, H, W), dtype=jnp.float32)
        s = 1.0 / np.sqrt(C)
        Wq = jax.random.normal(ks[1], (C, C), dtype=jnp.float32) * s
        bq = jax.random.normal(ks[2], (C,), dtype=jnp.float32) * 0.01
        Wk = jax.random.normal(ks[3], (C, C), dtype=jnp.float32) * s
        bk = jax.random.normal(ks[4], (C,), dtype=jnp.float32) * 0.01
        Wv = jax.random.normal(ks[5], (C, C), dtype=jnp.float32) * s
        bv = jax.random.normal(ks[6], (C,), dtype=jnp.float32) * 0.01
        return {'fuse': fuse, 'Wq': Wq, 'bq': bq, 'Wk': Wk, 'bk': bk, 'Wv': Wv, 'bv': bv}
    _L0_conv_all = _L0_conv_setup()
    _L0_conv_in = {k: v for k, v in _L0_conv_all.items() if k in ('Wq', 'bq', 'Wk', 'bk', 'Wv', 'bv', )}
    del _L0_conv_all

    def _L1_conv_setup():
        import jax, jax.numpy as jnp
        import numpy as np
        KERNEL = (3, 3)
        PADDING = (1, 1)
        STRIDE = (1, 1)
        IN_CHANNELS = 256
        OUT_CHANNELS = 256
        key = jax.random.key(seed)
        k1, k2 = jax.random.split(key)
        x = jax.random.normal(k1, (32, IN_CHANNELS, 56, 56), dtype=jnp.float32)
        w = jax.random.normal(k2, (IN_CHANNELS * KERNEL[0] * KERNEL[1], OUT_CHANNELS), dtype=jnp.float32) * 0.02
        return {'x': x, 'weight_matrix': w}
    _L1_conv_all = _L1_conv_setup()
    _L1_conv_in = {k: v for k, v in _L1_conv_all.items() if k in ('weight_matrix', )}
    del _L1_conv_all

    return {
        "x": x,
        "L0_conv_Wq": _L0_conv_in["Wq"],
        "L0_conv_bq": _L0_conv_in["bq"],
        "L0_conv_Wk": _L0_conv_in["Wk"],
        "L0_conv_bk": _L0_conv_in["bk"],
        "L0_conv_Wv": _L0_conv_in["Wv"],
        "L0_conv_bv": _L0_conv_in["bv"],
        "L1_conv_weight_matrix": _L1_conv_in["weight_matrix"],
    }

def reference(x, L0_conv_Wq, L0_conv_bq, L0_conv_Wk, L0_conv_bk, L0_conv_Wv, L0_conv_bv, L1_conv_weight_matrix):
    import jax
    import jax.numpy as jnp
    def _L0_conv_ref(fuse, Wq, bq, Wk, bk, Wv, bv):
        import jax, jax.numpy as jnp
        import numpy as np
        CUTOFF = 0.05

        def _freq_filter(x_chw, filter_type):
            x = jax.lax.stop_gradient(x_chw)
            C, H, W = x.shape
            a = jnp.abs(x)
            mn = a.min(axis=(1, 2), keepdims=True)
            ptp = a.max(axis=(1, 2), keepdims=True) - mn
            q = jnp.floor(255.0 * (a - mn) / ptp)
            f = jnp.fft.fftshift(jnp.fft.fft2(q), axes=(-2, -1))
            crow, ccol = (H // 2, W // 2)
            dr, dc = (int(CUTOFF * crow), int(CUTOFF * ccol))
            m = jnp.zeros((H, W), dtype=q.dtype)
            m = m.at[crow - dr:crow + dr, ccol - dc:ccol + dc].set(1.0)
            if filter_type == 'low_pass':
                m = 1.0 - m
            out = jnp.abs(jnp.fft.ifft2(jnp.fft.ifftshift(f * m, axes=(-2, -1))))
            return out.astype(x_chw.dtype)

        def _conv1x1(x, w, b):
            return jnp.einsum('oc,bchw->bohw', w, x) + b[None, :, None, None]
        B, C, H, W = fuse.shape
        scale = 1.0 / C ** 0.5
        FQ = jnp.broadcast_to(_freq_filter(fuse[0], 'high_pass'), fuse.shape)
        FK = jnp.broadcast_to(_freq_filter(fuse[0], 'low_pass'), fuse.shape)
        fuse_Query = _conv1x1(FQ, Wq, bq).reshape(B, C, H * W)
        fuse_Q_mask = fuse_Query.reshape(B * H, C * W)
        fuse_Query_t = jnp.transpose(fuse_Query, (0, 2, 1))
        fuse_Key = _conv1x1(FK, Wk, bk).reshape(B, C, H * W)
        Fuse_Q_mask = jnp.max(fuse_Q_mask, axis=0, keepdims=True)
        mask_KQ = jnp.einsum('bnc,bcm->bnm', fuse_Query_t, fuse_Key) * scale
        mask_KQ = jax.nn.softmax(mask_KQ, axis=0)
        mask_KQ = jnp.max(mask_KQ, axis=1)
        mask_KQ = mask_KQ.reshape(-1, W)
        mask_KQ = jnp.max(mask_KQ, axis=-1, keepdims=True)
        mask = (mask_KQ @ Fuse_Q_mask).reshape(B, C, H, W)
        fuse_Value = _conv1x1(fuse, Wv, bv)
        return fuse_Value + fuse_Value * mask

    def _L1_conv_ref(x, weight_matrix):
        import jax, jax.numpy as jnp
        import numpy as np
        KERNEL = (3, 3)
        PADDING = (1, 1)
        STRIDE = (1, 1)
        IN_CHANNELS = 256
        OUT_CHANNELS = 256
        kh, kw = KERNEL
        c_in = IN_CHANNELS
        c_out = weight_matrix.shape[1]
        w = weight_matrix.reshape(c_in, kh, kw, c_out).transpose(3, 0, 1, 2)
        out = jax.lax.conv_general_dilated(x, w, window_strides=STRIDE, padding=[(PADDING[0], PADDING[0]), (PADDING[1], PADDING[1])], dimension_numbers=('NCHW', 'OIHW', 'NCHW'))
        return out

    def _gn(v, G=32, eps=1e-5):
        B_, C_, H_, W_ = v.shape
        g = v.reshape(B_, G, C_ // G, H_, W_)
        m = jnp.mean(g, axis=(2, 3, 4), keepdims=True)
        s = jnp.var(g, axis=(2, 3, 4), keepdims=True)
        return ((g - m) / jnp.sqrt(s + eps)).reshape(v.shape)

    def _ln_c(v, eps=1e-6):
        m = jnp.mean(v, axis=1, keepdims=True)
        s = jnp.var(v, axis=1, keepdims=True)
        return (v - m) / jnp.sqrt(s + eps)

    def _ln_t(v, eps=1e-5):
        m = jnp.mean(v, axis=-1, keepdims=True)
        s = jnp.var(v, axis=-1, keepdims=True)
        return (v - m) / jnp.sqrt(s + eps)

    def _to_tokens(v):
        B_, C_, H_, W_ = v.shape
        return v.reshape(B_, C_, H_ * W_).transpose(0, 2, 1)
    def _from_tokens(t, like):
        B_, C_, H_, W_ = like.shape
        return t.transpose(0, 2, 1).reshape(B_, C_, H_, W_)

    x = x + _L0_conv_ref(_gn(x), L0_conv_Wq, L0_conv_bq, L0_conv_Wk, L0_conv_bk, L0_conv_Wv, L0_conv_bv)
    x = x + _L1_conv_ref(_gn(x), L1_conv_weight_matrix)
    return x


_drawn_inputs = setup_inputs


def setup_inputs(seed=0):
    import zlib

    import numpy as np

    out = dict(_drawn_inputs(seed))
    spreads = {}
    factors = {'L0_conv_bq': 8.0, 'L0_conv_bv': 5.405, 'L1_conv_weight_matrix': 6.83}
    for name, (base, spread) in spreads.items():
        noise = np.random.default_rng([zlib.crc32(name.encode()), seed]).standard_normal(out[name].shape)
        drawn = base * np.exp(spread * noise) if base else spread * noise
        out[name] = jnp.asarray(drawn.astype(out[name].dtype))
    for name, factor in factors.items():
        out[name] = (out[name] * factor).astype(out[name].dtype)
    return out
```

```python
from contextlib import ExitStack

import numpy as np

import concourse.bass as bass
from concourse import mybir

ALU = mybir.AluOpType
ACT = mybir.ActivationFunctionType
AX = mybir.AxisListType
F32 = mybir.dt.float32
F32R = mybir.dt.float32r
BF16 = mybir.dt.bfloat16
U16 = mybir.dt.uint16

P = 128
C, H, W = 256, 96, 96
HALVES = C // P
PIX = H * W
TILES = PIX // P
CHUNK = 512
CHUNKS = PIX // CHUNK
CT = CHUNK // P
PAIRS = CHUNKS // 2
GROUPS = 32
GC = C // GROUPS
MODS = 8
NB = 25
QCOLS = C * W // P
ROUND = 2.0 ** 23
LOADS = 6
LOADW = PIX // LOADS
EPS = 1e-5
SBLK = 32
SK = 3 * SBLK
HP, WP = H + 2, W + 2
CR = 4
CCH = H // CR
CW = CR * W


def frequency_tables():
    def f32r(a):
        b = a.astype(np.float32).view(np.uint32).astype(np.uint64)
        b = (b + 0x7FF + ((b >> 12) & 1)) & 0xFFFFF000
        return b.astype(np.uint32).view(np.float32)

    def bf16_bits(a):
        b = a.astype(np.float32).view(np.uint32).astype(np.uint64)
        return ((b + 0x7FFF + ((b >> 16) & 1)) >> 16).astype(np.uint16)

    def bf16_value(bits):
        return (bits.astype(np.uint32) << 16).view(np.float32).astype(np.float64)

    def basis(n):
        a = 2 * np.pi * np.arange(n) / n
        return np.stack([np.ones(n), np.cos(a), np.sin(a), np.cos(2 * a), np.sin(2 * a)])

    bh, bw = basis(H), basis(W)
    fwd = np.einsum("ih,jw->hwij", bh, bw).reshape(PIX, NB)
    table = np.zeros((PIX, 3, SBLK), np.uint16)
    rest = fwd
    for part in range(3):
        bits = bf16_bits(rest)
        table[:, part, :NB] = bits
        rest = rest - bf16_value(bits)
    forward = np.ascontiguousarray(table.reshape(TILES, P, SK).transpose(1, 0, 2))

    def even(b):
        return np.stack([b[0], 2 * b[1], 2 * b[2], b[3], b[4]])

    def odd(b):
        z = np.zeros_like(b[0])
        return np.stack([z, z, z, -b[4], b[3]])

    eh, ew, oh, ow = even(bh), even(bw), odd(bh), odd(bw)
    prod = lambda a, b: np.einsum("ih,jw->ijhw", a, b).reshape(NB, PIX) / PIX
    inverse = np.zeros((SK, CHUNKS, 2, CHUNK), np.float32)
    for part, g in enumerate((prod(eh, ew) - prod(oh, ow), prod(eh, ow) + prod(oh, ew))):
        hi = f32r(g)
        lo = f32r(g - hi)
        for block, v in enumerate((hi, lo, hi)):
            inverse[block * SBLK:block * SBLK + NB, :, part, :] = v.reshape(NB, CHUNKS, CHUNK)
    return forward, np.ascontiguousarray(inverse)


def small_constants():
    out = np.zeros((P, 2 * P + SK), np.float32)
    out[:, :P] = np.eye(P)
    out[:, P:2 * P] = np.kron(np.eye(P // GC), np.full((GC, GC), 1.0 / GC))
    for a in range(3):
        for b in range(3):
            for r in range(NB):
                out[a * SBLK + r, 2 * P + b * SBLK + r] = 1.0
    return out


def peeled(eng, count, body):
    body(0, True)
    with eng.Fori(1, count) as i:
        body(i, False)


def build(nc, x, wqT, bq, wvT, bv, wconv, forward, inverse, consts, out):
    ctx = ExitStack()
    with ctx:
        def sb(name, shape, dt=F32):
            return ctx.enter_context(nc.sbuf_tensor(name, shape, dt))

        def sem(name):
            return ctx.enter_context(nc.semaphore(name))

        region_a = sb("region_a", [P, HALVES * HP * WP])
        xn = region_a[:, 0:HALVES * PIX].rearrange("p (a n) -> p a n", a=HALVES)
        padded = region_a[:, :].rearrange("p (a h w) -> p a h w", a=HALVES, h=HP)
        value = sb("value", [P, HALVES, PIX])
        region_w = sb("region_w", [P, HALVES * 9 * C])
        wc = region_w[:, :].rearrange("p (a t o) -> p a t o", a=HALVES, t=9)
        fwd_words = TILES * SK // 2
        fwd_u16 = region_w[:, 0:fwd_words].bitcast(U16)
        fwd_sb = region_w[:, 0:fwd_words].bitcast(BF16)
        qmax = region_w[:, fwd_words:fwd_words + MODS * TILES]
        mask_px = region_w[:, fwd_words + MODS * TILES:fwd_words + 2 * MODS * TILES]
        scratch = sb("scratch", [P, 6144])
        absx = scratch[:, 0:1024].rearrange("p (u n) -> p u n", u=2)
        level = scratch[:, 1024:2048].rearrange("p (u n) -> p u n", u=2)
        nearest = scratch[:, 2048:2560].bitcast(BF16).rearrange("p (u n) -> p u n", u=2)
        above = scratch[:, 2560:3072].bitcast(BF16).rearrange("p (u n) -> p u n", u=2)
        qT = scratch[:, 3072:3584].bitcast(BF16).rearrange("p (u n) -> p u n", u=2)
        wv_sb = scratch[:, 5632:6144].rearrange("p (a o) -> p a o", a=HALVES)
        bq_rows = scratch[:, 3584:3840]
        bq_rest = scratch[:, 3840:4096]
        sums_sb = scratch[:, 4096:4352]
        table_ring = sb("table_ring", [SK, 2, 2, CHUNK], F32R)
        sq_re = scratch[:, 0:1024].rearrange("p (u n) -> p u n", u=2)
        sq_im = scratch[:, 1024:2048].rearrange("p (u n) -> p u n", u=2)
        fq = scratch[:, 2048:4096].rearrange("p (u a n) -> p u a n", u=2, a=HALVES)
        x_ring = scratch[:, 0:2048].rearrange("p (u a n) -> p u a n", u=2, a=HALVES)
        mask_rep = scratch[:, 2048:3072].rearrange("p (u t g k) -> p u t g k", u=2, t=CT, k=MODS)
        wq_sb = sb("wq_sb", [P, HALVES, C])
        cst = sb("cst", [P, 2 * P + SK])
        ident, group_mean, stacker = cst[:, 0:P], cst[:, P:2 * P], cst[0:SK, 2 * P:2 * P + SK]
        ident_b = sb("ident_b", [P, 2, P], BF16)
        ones_b = sb("ones_b", [SK, P], BF16)
        bq_parts = sb("bq_parts", [SK, C], BF16)
        bq_cast = sb("bq_cast", [SK, C], BF16)
        stacked = sb("stacked", [SK, C], F32R)
        bv_sb = sb("bv_sb", [P, HALVES])
        stats = sb("stats", [P, HALVES, CHUNKS, 6])
        mv = sb("mv", [P, HALVES, 2])
        gn_t = sb("gn_t", [P, 8, HALVES])
        rstd = sb("rstd", [P, 2, HALVES])
        nbias = sb("nbias", [P, 2, HALVES])
        ext = sb("ext", [P, 2, CHUNKS])
        qz = sb("qz", [P, 6, HALVES])

        banks = [ctx.enter_context(nc.psum_tensor(f"bank{i}", [P, CHUNK], F32)) for i in range(4)]
        quad = ctx.enter_context(nc.psum_tensor("quad", [P, 4, CHUNK], F32))
        qT_ps = banks[0:2]
        sums_ps = banks[2]
        small_ps = banks[3]
        v_ps = quad
        field_ps = banks
        query_ps = quad
        mask_ps = banks[0:2]
        conv_ps = quad

        s_x = [[sem(f"x_in{a}_{i}") for i in range(LOADS)] for a in range(HALVES)]
        s_cst, s_wv, s_bias, s_fwd, s_wq, s_wc = (sem(n) for n in (
            "cst_in", "wv_in", "bias_in", "fwd_in", "wq_in", "wconv_in"))
        s_table = [sem("table_in0"), sem("table_in1")]
        s_xr = [sem("x_again0"), sem("x_again1")]
        dve_step = sem("dve_step")
        s_prep = sem("prep_done")
        s_ident = sem("bf16_identities")
        s_gps = sem("group_psum")
        s_gin = sem("group_in")
        s_var = sem("variance_ready")
        s_std = sem("std_ready")
        s_norm = sem("norm_ready")
        s_xn = sem("xn_ready")
        s_ext = sem("extrema_ready")
        s_qz = sem("level_scale_ready")
        s_abs, s_level, s_near, s_quant = (sem(n) for n in (
            "abs_ready", "level_ready", "nearest_ready", "quantised"))
        s_T, s_qT, s_dft = sem("transposed"), sem("qT_ready"), sem("sums_added")
        s_v, s_vout = sem("v_product"), sem("v_ready")
        s_ssb, s_stack_ps, s_stack = (sem(n) for n in ("sums_copied", "sums_stacked_psum", "sums_stacked"))
        s_field, s_sq, s_pow, s_fq = (sem(n) for n in (
            "field_ready", "squares_ready", "power_ready", "fq_ready"))
        s_query, s_qmax = sem("query_ready"), sem("query_reduced")
        s_mask, s_rep, s_mT = sem("mask_ready"), sem("mask_spread"), sem("mask_transposed")
        s_gain, s_x1, s_stat2 = sem("gained"), sem("x1_ready"), sem("x1_counted")
        s_pad, s_rows = sem("pad_zero"), sem("rows_normalised")
        s_conv, s_out_sb, s_stored = sem("conv_ready"), sem("out_ready"), sem("out_stored")

        block = ctx.enter_context(nc.Block())

        def chunk(i, u):
            return bass.ds((2 * i + u) * CHUNK, CHUNK)

        @block.sync
        def _(sp):
            for a in range(HALVES):
                for i in range(LOADS):
                    sp.dma_start(xn[:, a, i * LOADW:(i + 1) * LOADW],
                                 x[a * P:(a + 1) * P, i * LOADW:(i + 1) * LOADW]).then_inc(s_x[a][i], 16)
                if a == 0:
                    sp.dma_start(cst[:, :], consts).then_inc(s_cst, 16)
            sp.dma_start(fwd_u16, forward.rearrange("p t k -> p (t k)")).then_inc(s_fwd, 16)
            sp.dma_start(wv_sb, wvT.rearrange("(a p) o -> p a o", p=P)).then_inc(s_wv, 16)
            sp.dma_start(wq_sb[:, :, :], wqT.rearrange("(a p) o -> p a o", p=P)).then_inc(s_wq, 16)
            sp.dma_start(bv_sb[:, :], bv).then_inc(s_bias, 16)
            sp.wait_ge(s_prep, 3)
            for r in range(3):
                sp.dma_start(bq_rows[r * SBLK:r * SBLK + 1, :], bq.rearrange("(a n) -> a n", a=1)
                             ).then_inc(s_bias, 16)

            def x_again(i, first):
                for u in range(2):
                    if not first:
                        sp.wait_ge(s_x1, 4 * i + 2 * u - 2)
                    sp.dma_start(x_ring[:, u], x.rearrange("(a p) n -> p a n", p=P)[:, :, chunk(i, u)]
                                 ).then_inc(s_xr[u], 16)

            sp.wait_ge(s_fq, 2 * CHUNKS)
            peeled(sp, PAIRS, x_again)
            sp.wait_ge(s_rep, CHUNKS)
            sp.dma_start(wc.rearrange("p a t o -> p a (t o)"),
                         wconv.rearrange("(a p) n -> p a n", p=P)).then_inc(s_wc, 16)
            with sp.Fori(0, CCH) as i:
                sp.wait_ge(s_out_sb, 2 * i + 2)
                sp.dma_start(out.rearrange("(a p) n -> p a n", p=P)[:, :, bass.ds(i * CW, CW)],
                             value[:, :, bass.ds(i * CW, CW)]).then_inc(s_stored, 16)
            sp.wait_ge(s_stored, 16 * CCH)

        @block.gpsimd
        def _(pool):
            pool.memset(bq_rows[0:SK, :], 0.0).then_inc(s_prep, 1)
            pool.memset(ones_b[:, :], 1.0).then_inc(s_prep, 1)
            pool.memset(bq_parts[:, :], 0.0).then_inc(s_prep, 1)

            def table(i, first):
                for u in range(2):
                    if not first:
                        pool.wait_ge(s_field, 4 * i + 2 * u - 2)
                    pool.dma_start(table_ring[:, u], inverse[:, bass.ds(2 * i + u, 1)].rearrange(
                        "k o f n -> k (o f) n")).then_inc(s_table[u], 16)

            peeled(pool, PAIRS, table)
            with pool.Fori(0, PAIRS) as i:
                for u in range(2):
                    pool.wait_ge(s_xr[u], 16 * (i + 1))
                    for a in range(HALVES):
                        pool.wait_ge(s_gain, 4 * i + 2 * u + a + 1)
                        v = value[:, a, chunk(i, u)]
                        pool.tensor_tensor(v, v, x_ring[:, u, a], ALU.add).then_inc(s_x1, 1)
            pool.memset(padded[:, :, 0, :], 0.0).then_inc(s_pad, 1)
            pool.memset(padded[:, :, HP - 1, :], 0.0).then_inc(s_pad, 1)
            pool.memset(padded[:, :, 1:HP - 1, 0:1], 0.0).then_inc(s_pad, 1)
            pool.memset(padded[:, :, 1:HP - 1, WP - 1:WP], 0.0).then_inc(s_pad, 1)

        @block.scalar
        def _(act):
            def std(n, lo, hi):
                act.wait_ge(s_var, n)
                act.activation(gn_t[:, 4, lo:hi], gn_t[:, 3, lo:hi], ACT.Sqrt).then_inc(s_std, 1)

            def normalise(a):
                act.wait_ge(s_norm, a + 1)
                with act.Fori(0, LOADS) as c:
                    v = xn[:, a, bass.ds(c * LOADW, LOADW)]
                    act.activation(v, v, ACT.Identity, bias=nbias[:, 0, a:a + 1],
                                   scale=rstd[:, 0, a:a + 1]).then_inc(s_xn, 1)

            def levels(a, n, i, first):
                for u in range(2):
                    if not first:
                        act.wait_ge(s_level, 2 * n + u - 1)
                    act.activation(absx[:, u], xn[:, a, chunk(i, u)], ACT.Abs).then_inc(s_abs, 1)
                for u in range(2):
                    act.wait_ge(s_abs, 2 * n + u + 1)
                    if not first:
                        act.wait_ge(s_quant, 2 * n + u - 1)
                    act.activation(level[:, u], absx[:, u], ACT.Relu, bias=qz[:, 4, a:a + 1],
                                   scale=qz[:, 3, a:a + 1]).then_inc(s_level, 1)

            def qT_copy(n, first):
                for u in range(2):
                    act.wait_ge(s_T, 2 * n + u + 1)
                    if not first:
                        act.wait_ge(s_dft, 2 * n + u - 1)
                    act.activation(qT[:, u], qT_ps[u][:, :], ACT.Copy).then_inc(s_qT, 1)

            def v_copy(i):
                for u in range(2):
                    act.wait_ge(s_v, 2 * i + u + 1)
                    for m in range(HALVES):
                        act.activation(value[:, m, chunk(i, u)], v_ps[:, 2 * u + m], ACT.Identity,
                                       bias=bv_sb[:, m:m + 1]).then_inc(s_vout, 1)

            std(1, 0, 1)
            normalise(0)
            std(2, 1, 2)
            normalise(1)
            act.wait_ge(s_qz, 1)
            levels(0, 0, 0, True)
            levels(0, 1, 1, False)
            qT_copy(0, True)
            with act.Fori(2, PAIRS) as i:
                levels(0, i, i, False)
                qT_copy(i - 1, False)
            qT_copy(PAIRS - 1, False)
            act.wait_ge(s_qz, 2)
            act.wait_ge(s_bias, 16 * 4)
            levels(1, PAIRS, 0, False)
            with act.Fori(1, PAIRS) as i:
                levels(1, i + PAIRS, i, False)
                v_copy(i - 1)
                qT_copy(i + (PAIRS - 1), False)
            v_copy(PAIRS - 1)
            qT_copy(2 * PAIRS - 1, False)

            def squares(n, a, first=False):
                act.wait_ge(s_field, n + 1)
                act.activation(sq_im[:, a], field_ps[2 * a + 1][:, :], ACT.Square).then_inc(s_sq, 1)
                if not first:
                    act.wait_ge(s_fq, n - 1)
                act.activation(sq_re[:, a], field_ps[2 * a][:, :], ACT.Square).then_inc(s_sq, 1)

            def root(i, u, a, first):
                act.wait_ge(s_pow, 4 * i + 2 * u + a + 1)
                if not first:
                    act.wait_ge(s_query, 2 * i + u - 1)
                act.activation(fq[:, u, a], sq_re[:, a], ACT.Sqrt).then_inc(s_fq, 1)

            def moduli(i, first, last=False):
                for u in range(2):
                    for a in range(HALVES):
                        root(i, u, a, first)
                        if u == 0 or not last:
                            squares(4 * i + 2 * u + a + 2, a)

            squares(0, 0, True)
            squares(1, 1, True)
            moduli(0, True)
            with act.Fori(1, PAIRS - 1) as i:
                moduli(i, False)
            moduli(PAIRS - 1, False, True)

            def spread(i, first):
                for u in range(2):
                    if not first:
                        act.wait_ge(s_mT, 2 * i + u - 1)
                    src = mask_px[:, bass.ds((2 * i + u) * CT * MODS, CT * MODS)].rearrange(
                        "p (t g k) -> p t g k", t=CT, g=1).broadcast_to([P, CT, P // MODS, MODS])
                    act.activation(mask_rep[:, u], src, ACT.Copy).then_inc(s_rep, 1)

            act.wait_ge(s_mask, 1)
            peeled(act, PAIRS, spread)
            std(3, 0, 2)
            act.wait_ge(s_norm, 3)
            act.wait_ge(s_pad, 4)
            with act.Fori(0, CCH) as i:
                for a in range(HALVES):
                    act.activation(padded[:, a, bass.ds(i * CR + 1, CR), 1:W + 1],
                                   value[:, a, bass.ds(i * CW, CW)].rearrange("p (h w) -> p h w", w=W),
                                   ACT.Identity, bias=nbias[:, 1, a:a + 1],
                                   scale=rstd[:, 1, a:a + 1]).then_inc(s_rows, 1)

        @block.tensor
        def _(pe):
            def group_sums(n, lo, hi):
                pe.wait_ge(s_gin, 2 * n + 1)
                pe.matmul(small_ps[:, 8 * n:8 * n + hi - lo], group_mean, mv[:, lo:hi, 0],
                          start=True, stop=True).then_inc(s_gps, 1)
                pe.wait_ge(s_gin, 2 * n + 2)
                pe.matmul(small_ps[:, 8 * n + 4:8 * n + 4 + hi - lo], group_mean, gn_t[:, 2, lo:hi],
                          start=True, stop=True).then_inc(s_gps, 1)

            def transposes(n, first):
                for u in range(2):
                    pe.wait_ge(s_quant, 2 * n + u + 1)
                    if not first:
                        pe.wait_ge(s_qT, 2 * n + u - 1)
                    for t in range(CT):
                        o = qT_ps[u][:, t * P:(t + 1) * P]
                        pe.matmul(o, nearest[:, u, t * P:(t + 1) * P], ident_b[:, 0, :], start=True, stop=False)
                        last = pe.matmul(o, above[:, u, t * P:(t + 1) * P], ident_b[:, 1, :],
                                         start=False, stop=True)
                    last.then_inc(s_T, 1)

            def sums(a, n, i, start=False, stop=False):
                for u in range(2):
                    pe.wait_ge(s_qT, 2 * n + u + 1)
                    for t in range(CT):
                        last = pe.matmul(sums_ps[0:SK, a * P:(a + 1) * P],
                                         fwd_sb[:, bass.ds(((2 * i + u) * CT + t) * SK, SK)],
                                         qT[:, u, t * P:(t + 1) * P],
                                         start=start and u == 0 and t == 0,
                                         stop=stop and u == 1 and t == CT - 1)
                    last.then_inc(s_dft, 1)

            def v_product(i, first):
                for u in range(2):
                    for m in range(HALVES):
                        if not first:
                            pe.wait_ge(s_vout, 4 * i + 2 * u + m - 3)
                        for k in range(HALVES):
                            last = pe.matmul(v_ps[:, 2 * u + m], wv_sb[:, k, m * P:(m + 1) * P],
                                             xn[:, k, chunk(i, u)], start=k == 0, stop=k == HALVES - 1)
                    last.then_inc(s_v, 1)

            pe.wait_ge(s_cst, 16)
            group_sums(0, 0, 1)
            group_sums(1, 1, 2)
            pe.wait_ge(s_ident, 1)
            pe.wait_ge(s_fwd, 16)
            transposes(0, True)
            transposes(1, False)
            sums(0, 0, 0, start=True)
            with pe.Fori(2, PAIRS) as i:
                transposes(i, False)
                sums(0, i - 1, i - 1)
            sums(0, PAIRS - 1, PAIRS - 1, stop=True)
            pe.wait_ge(s_wv, 16)
            pe.wait_ge(s_xn, 2 * LOADS)
            v_product(0, True)
            transposes(PAIRS, False)
            v_product(1, False)
            transposes(PAIRS + 1, False)
            sums(1, PAIRS, 0, start=True)
            with pe.Fori(2, PAIRS) as i:
                v_product(i, False)
                transposes(i + PAIRS, False)
                sums(1, i + (PAIRS - 1), i - 1)
            sums(1, 2 * PAIRS - 1, PAIRS - 1, stop=True)
            pe.wait_ge(s_ssb, 1)
            pe.matmul(small_ps[0:SK, 0:C], stacker, sums_sb[0:SK, :], start=True, stop=True).then_inc(s_stack_ps, 1)

            def fields(i, u, first):
                pe.wait_ge(s_table[u], 16 * (i + 1))
                for a in range(HALVES):
                    if not first:
                        pe.wait_ge(s_sq, 8 * i + 4 * u + 2 * a - 2)
                    for part in range(2):
                        last = pe.matmul(field_ps[2 * a + part][:, :], stacked[:, a * P:(a + 1) * P],
                                         table_ring[:, u, part], start=True, stop=True)
                    last.then_inc(s_field, 1)

            def query(i, u, first):
                pe.wait_ge(s_fq, 4 * i + 2 * u + 2)
                if not first:
                    pe.wait_ge(s_qmax, 2 * i + u - 1)
                for t in range(CT):
                    o = query_ps[:, 2 * u + t // 2, (t % 2) * C:(t % 2 + 1) * C]
                    for a in range(HALVES):
                        pe.matmul(o, fq[:, u, a, t * P:(t + 1) * P], wq_sb[:, a, :], start=a == 0, stop=False)
                    last = pe.matmul(o, ones_b[:, :], bq_parts[:, :], start=False, stop=True)
                last.then_inc(s_query, 1)

            pe.wait_ge(s_stack, 1)
            pe.wait_ge(s_wq, 16)
            pe.wait_ge(s_vout, 2 * CHUNKS)
            fields(0, 0, True)
            fields(0, 1, False)
            query(0, 0, True)
            fields(1, 0, False)
            query(0, 1, True)
            with pe.Fori(1, PAIRS - 1) as i:
                fields(i, 1, False)
                query(i, 0, False)
                fields(i + 1, 0, False)
                query(i, 1, False)
            fields(PAIRS - 1, 1, False)
            query(PAIRS - 1, 0, False)
            query(PAIRS - 1, 1, False)

            def mask_transposes(i, first):
                for u in range(2):
                    pe.wait_ge(s_rep, 2 * i + u + 1)
                    if not first:
                        pe.wait_ge(s_gain, 4 * i + 2 * u - 2)
                    for t in range(CT):
                        last = pe.transpose(mask_ps[u][:, t * P:(t + 1) * P],
                                            mask_rep[:, u, t].rearrange("p g k -> p (g k)"), ident)
                    last.then_inc(s_mT, 1)

            peeled(pe, PAIRS, mask_transposes)
            group_sums(2, 0, 2)

            def conv(i, u, first, rows):
                pe.wait_ge(s_rows, rows)
                for m in range(HALVES):
                    if not first:
                        pe.wait_ge(s_out_sb, 4 * i + 2 * u + m - 3)
                    for k in range(HALVES):
                        for tap in range(9):
                            last = pe.matmul(conv_ps[:, 2 * u + m, 0:CW], wc[:, k, tap, m * P:(m + 1) * P],
                                             padded[:, k, bass.ds((2 * i + u) * CR + tap // 3, CR),
                                                    tap % 3:tap % 3 + W],
                                             start=k == 0 and tap == 0, stop=k == HALVES - 1 and tap == 8)
                    last.then_inc(s_conv, 1)

            pe.wait_ge(s_wc, 16)
            pe.wait_ge(s_pad, 4)
            conv(0, 0, True, 4)
            conv(0, 1, True, 6)
            with pe.Fori(1, CCH // 2 - 1) as i:
                conv(i, 0, False, 4 * i + 4)
                conv(i, 1, False, 4 * i + 6)
            conv(CCH // 2 - 1, 0, False, 2 * CCH)
            conv(CCH // 2 - 1, 1, False, 2 * CCH)

        @block.vector
        def _(dve):
            steps = [0]

            def step(ins):
                steps[0] += 1
                ins.then_inc(dve_step, 1)
                dve.wait_ge(dve_step, steps[0])

            def group_norm(layer, n, lo, hi):
                w = hi - lo
                row = [gn_t[:, j, lo:hi] for j in range(8)]
                for a in range(lo, hi):
                    ins = dve.bn_aggr(mv[:, a, :], stats[:, a].rearrange("p c s -> p (c s)"))
                ins.then_inc(s_gin, 1)
                dve.wait_ge(s_gin, 2 * n + 1)
                dve.wait_ge(s_gps, 2 * n + 1)
                mean = small_ps[:, 8 * n:8 * n + w]
                step(dve.tensor_tensor(row[0], mv[:, lo:hi, 0], mean, ALU.subtract))
                step(dve.tensor_copy(row[1], mean))
                step(dve.tensor_tensor(row[2], row[0], row[0], ALU.mult))
                dve.tensor_tensor(row[2], row[2], mv[:, lo:hi, 1], ALU.add).then_inc(s_gin, 1)
                dve.wait_ge(s_gps, 2 * n + 2)
                dve.tensor_scalar(row[3], small_ps[:, 8 * n + 4:8 * n + 4 + w], EPS, None, ALU.add
                                  ).then_inc(s_var, 1)
                dve.wait_ge(s_std, n + 1)
                dve.wait_ge(s_var, n + 1)
                step(dve.reciprocal(row[5], row[4]))
                step(dve.tensor_tensor(row[6], row[5], row[5], ALU.mult))
                step(dve.tensor_tensor(row[6], row[6], row[3], ALU.mult))
                step(dve.tensor_scalar(row[6], row[6], -0.5, 1.5, ALU.mult, ALU.add))
                step(dve.tensor_tensor(rstd[:, layer, lo:hi], row[5], row[6], ALU.mult))
                dve.scalar_tensor_tensor(nbias[:, layer, lo:hi], row[1], -1.0, rstd[:, layer, lo:hi],
                                         ALU.mult, ALU.mult).then_inc(s_norm, 1)

            def half_stats(a):
                for i in range(LOADS):
                    dve.wait_ge(s_x[a][i], 16)
                    for j in range(LOADW // CHUNK):
                        ins = dve.bn_stats(stats[:, a, i * (LOADW // CHUNK) + j],
                                           xn[:, a, i * LOADW + j * CHUNK:i * LOADW + (j + 1) * CHUNK])
                step(ins)

            def extrema(a):
                with dve.Fori(0, LOADS) as c:
                    dve.wait_ge(s_xn, c + (1 + a * LOADS))
                    for j, op in enumerate((ALU.max, ALU.min)):
                        dve.tensor_reduce(ext[:, j, bass.ds(c, 1)], xn[:, a, bass.ds(c * LOADW, LOADW)], AX.X, op,
                                          apply_absolute_value=True).then_inc(s_ext, 1)
                dve.wait_ge(s_ext, 2 * LOADS * (a + 1))
                z = [qz[:, j, a:a + 1] for j in range(6)]
                step(dve.tensor_reduce(z[0], ext[:, 0, 0:LOADS], AX.X, ALU.max))
                step(dve.tensor_reduce(z[1], ext[:, 1, 0:LOADS], AX.X, ALU.min))
                step(dve.tensor_tensor(z[2], z[0], z[1], ALU.subtract))
                step(dve.reciprocal(z[5], z[2]))
                step(dve.tensor_scalar(z[3], z[5], 255.0 * (1.0 + 2.0 ** -22), None, ALU.mult))
                dve.scalar_tensor_tensor(z[4], z[1], -1.0, z[3], ALU.mult, ALU.mult).then_inc(s_qz, 1)

            def quantise(n, first):
                for u in range(2):
                    dve.wait_ge(s_level, 2 * n + u + 1)
                    if not first:
                        dve.wait_ge(s_T, 2 * n + u - 1)
                    dve.tensor_scalar(nearest[:, u], level[:, u], ROUND, -ROUND, ALU.add, ALU.add
                                      ).then_inc(s_near, 1)
                for u in range(2):
                    dve.wait_ge(s_near, 2 * n + u + 1)
                    dve.tensor_tensor(above[:, u], level[:, u], nearest[:, u], ALU.is_lt).then_inc(s_quant, 1)

            half_stats(0)
            group_norm(0, 0, 0, 1)
            half_stats(1)
            group_norm(0, 1, 1, 2)
            for j, sign in enumerate((1.0, -1.0)):
                ins = dve.tensor_scalar(ident_b[:, j], ident, sign, None, ALU.mult)
            ins.then_inc(s_ident, 1)
            extrema(0)
            peeled(dve, PAIRS, quantise)
            extrema(1)
            with dve.Fori(PAIRS, 2 * PAIRS) as n:
                quantise(n, False)

            dve.wait_ge(s_bias, 16 * 4)
            for part in range(3):
                rows = slice(part * SBLK, part * SBLK + 1)
                src = bq_rows if part == 0 else bq_rest
                step(dve.tensor_copy(bq_cast[:, :], src[0:SK, :]))
                step(dve.tensor_copy(bq_parts[rows, :], bq_cast[rows, :]))
                if part < 2:
                    step(dve.tensor_tensor(bq_rest[0:SK, :], src[0:SK, :], bq_cast[:, :], ALU.subtract))

            dve.wait_ge(s_dft, 4 * PAIRS)
            dve.tensor_copy(sums_sb[0:SK, :], sums_ps[0:SK, 0:C]).then_inc(s_ssb, 1)
            dve.wait_ge(s_stack_ps, 1)
            step(dve.tensor_copy(stacked[:, :], small_ps[0:SK, 0:C]))
            lo = slice(2 * SBLK, SK)
            dve.tensor_tensor(stacked[lo, :], small_ps[lo, 0:C], stacked[lo, :].bitcast(F32), ALU.subtract
                              ).then_inc(s_stack, 1)

            def power(n, a):
                dve.wait_ge(s_sq, 2 * n + 2)
                dve.tensor_tensor(sq_re[:, a], sq_re[:, a], sq_im[:, a], ALU.add).then_inc(s_pow, 1)

            def query_max(i, u):
                dve.wait_ge(s_query, 2 * i + u + 1)
                src = query_ps[:, 2 * u:2 * u + 2, :].rearrange("p b (t c k) -> p k (b t) c", t=2, k=MODS)
                dst = qmax.rearrange("p (k t) -> p k t", k=MODS)[:, :, bass.ds((2 * i + u) * CT, CT)]
                dve.tensor_reduce(dst, src, AX.X, ALU.max).then_inc(s_qmax, 1)

            power(0, 0)
            power(1, 1)
            with dve.Fori(0, PAIRS - 1) as i:
                for u in range(2):
                    for a in range(HALVES):
                        power(4 * i + 2 * u + a + 2, a)
                    query_max(i, u)
            for a in range(HALVES):
                power(4 * (PAIRS - 1) + a + 2, a)
            query_max(PAIRS - 1, 0)
            query_max(PAIRS - 1, 1)
            dve.wait_ge(s_qmax, CHUNKS)
            for r in range(1, MODS * TILES // QCOLS):
                step(dve.tensor_tensor(qmax[:, 0:QCOLS], qmax[:, 0:QCOLS], qmax[:, r * QCOLS:(r + 1) * QCOLS],
                                       ALU.max))
            by_tile = mask_px.rearrange("p (t k) -> p k t", k=MODS)
            for k in range(MODS):
                t = 0
                while t < TILES:
                    col = (TILES * k + t) % QCOLS
                    n = min(TILES - t, QCOLS - col)
                    ins = dve.tensor_copy(by_tile[:, k, t:t + n], qmax[:, col:col + n])
                    t += n
            ins.then_inc(s_mask, 1)

            def gain(i, u, a):
                v = value[:, a, chunk(i, u)]
                dve.scalar_tensor_tensor(v, mask_ps[u][:, :], 1.0, v, ALU.add, ALU.mult).then_inc(s_gain, 1)

            def x1_stats(i, u):
                for a in range(HALVES):
                    dve.wait_ge(s_x1, 4 * i + 2 * u + a + 1)
                    dve.bn_stats(stats[:, a, bass.ds(2 * i + u, 1)].rearrange("p o s -> p (o s)"),
                                 value[:, a, chunk(i, u)]).then_inc(s_stat2, 1)

            def gains(i, u):
                dve.wait_ge(s_mT, 2 * i + u + 1)
                for a in range(HALVES):
                    gain(i, u, a)

            gains(0, 0)
            with dve.Fori(0, PAIRS - 1) as i:
                gains(i, 1)
                x1_stats(i, 0)
                gains(i + 1, 0)
                x1_stats(i, 1)
            gains(PAIRS - 1, 1)
            x1_stats(PAIRS - 1, 0)
            x1_stats(PAIRS - 1, 1)
            dve.wait_ge(s_stat2, 2 * CHUNKS)
            group_norm(1, 2, 0, 2)

            with dve.Fori(0, CCH // 2) as i:
                for u in range(2):
                    for m in range(HALVES):
                        dve.wait_ge(s_conv, 4 * i + 2 * u + m + 1)
                        o = value[:, m, bass.ds((2 * i + u) * CW, CW)]
                        dve.tensor_tensor(o, o, conv_ps[:, 2 * u + m, 0:CW], ALU.add).then_inc(s_out_sb, 1)


def kernel(x, L0_conv_Wq, L0_conv_bq, L0_conv_Wk, L0_conv_bk, L0_conv_Wv, L0_conv_bv, L1_conv_weight_matrix):
    import concourse.bacc as bacc
    from concourse.bass_utils import run_bass_kernel_spmd

    forward, inverse = frequency_tables()
    arrays = {
        "x": np.ascontiguousarray(np.asarray(x).reshape(C, PIX)),
        "wqT": np.ascontiguousarray(np.asarray(L0_conv_Wq).T),
        "bq": np.asarray(L0_conv_bq),
        "wvT": np.ascontiguousarray(np.asarray(L0_conv_Wv).T),
        "bv": np.ascontiguousarray(np.asarray(L0_conv_bv).reshape(HALVES, P).T),
        "wconv": np.ascontiguousarray(np.asarray(L1_conv_weight_matrix).reshape(C, 9 * C)),
        "forward": forward,
        "inverse": inverse,
        "consts": small_constants(),
    }
    nc = bacc.Bacc("TRN2", target_bir_lowering=False, num_devices=1)
    aps = {n: nc.dram_tensor(n, a.shape, mybir.dt.from_np(a.dtype), kind="ExternalInput").ap()
           for n, a in arrays.items()}
    out = nc.dram_tensor("out", (C, PIX), F32, kind="ExternalOutput").ap()
    build(nc, **aps, out=out)
    got = run_bass_kernel_spmd(nc, [arrays], core_ids=[0])
    return got.results[0]["out"].reshape(1, C, H, W)
```

```python
from contextlib import ExitStack

import numpy as np

import concourse.bass as bass
from concourse import mybir

ALU = mybir.AluOpType
ACT = mybir.ActivationFunctionType
AX = mybir.AxisListType
F32 = mybir.dt.float32
F32R = mybir.dt.float32r
BF16 = mybir.dt.bfloat16
U16 = mybir.dt.uint16

P = 128
C, H, W = 256, 96, 96
HALVES = C // P
PIX = H * W
TILES = PIX // P
CHUNK = 512
CHUNKS = PIX // CHUNK
CT = CHUNK // P
PAIRS = CHUNKS // 2
VLEAD = CHUNKS - PAIRS
GROUPS = 32
GC = C // GROUPS
MODS = 8
NB = 25
QCOLS = C * W // P
ROUND = 2.0 ** 23
LOADS = 6
LOADW = PIX // LOADS
EPS = 1e-5
SBLK = 32
SK = 3 * SBLK
NK = 3 * HALVES
POS = 6
WT = 4
CR = 16
TR = CR // WT
CCH = H // CR
CW = CR * W
XR = CR + 2
VS = 3
YS = 20


def frequency_tables():
    def f32r(a):
        b = a.astype(np.float32).view(np.uint32).astype(np.uint64)
        b = (b + 0x7FF + ((b >> 12) & 1)) & 0xFFFFF000
        return b.astype(np.uint32).view(np.float32)

    def bf16_bits(a):
        b = a.astype(np.float32).view(np.uint32).astype(np.uint64)
        return ((b + 0x7FFF + ((b >> 16) & 1)) >> 16).astype(np.uint16)

    def bf16_value(bits):
        return (bits.astype(np.uint32) << 16).view(np.float32).astype(np.float64)

    def basis(n):
        a = 2 * np.pi * np.arange(n) / n
        return np.stack([np.ones(n), np.cos(a), np.sin(a), np.cos(2 * a), np.sin(2 * a)])

    bh, bw = basis(H), basis(W)
    fwd = np.einsum("ih,jw->hwij", bh, bw).reshape(PIX, NB)
    table = np.zeros((PIX, 3, SBLK), np.uint16)
    rest = fwd
    for part in range(3):
        bits = bf16_bits(rest)
        table[:, part, :NB] = bits
        rest = rest - bf16_value(bits)
    forward = np.ascontiguousarray(table.reshape(TILES, P, SK).transpose(1, 0, 2))

    def even(b):
        return np.stack([b[0], 2 * b[1], 2 * b[2], b[3], b[4]])

    def odd(b):
        z = np.zeros_like(b[0])
        return np.stack([z, z, z, -b[4], b[3]])

    eh, ew, oh, ow = even(bh), even(bw), odd(bh), odd(bw)
    prod = lambda a, b: np.einsum("ih,jw->ijhw", a, b).reshape(NB, PIX) / PIX
    inverse = np.zeros((SK, CHUNKS, 2, CHUNK), np.float32)
    for part, g in enumerate((prod(eh, ew) - prod(oh, ow), prod(eh, ow) + prod(oh, ew))):
        hi = f32r(g)
        lo = f32r(g - hi)
        for block, v in enumerate((hi, lo, hi)):
            inverse[block * SBLK:block * SBLK + NB, :, part, :] = v.reshape(NB, CHUNKS, CHUNK)
    return forward, np.ascontiguousarray(inverse)


def small_constants():
    out = np.zeros((P, 2 * P + SK), np.float32)
    out[:, :P] = np.eye(P)
    out[:, P:2 * P] = np.kron(np.eye(P // GC), np.full((GC, GC), 1.0 / GC))
    for a in range(3):
        for b in range(3):
            for r in range(NB):
                out[a * SBLK + r, 2 * P + b * SBLK + r] = 1.0
    return out


def peeled(eng, count, body):
    body(0, True)
    with eng.Fori(1, count) as i:
        body(i, False)


def alternating(eng, body):
    body(0, 0, 0)
    body(1, 1, 0)
    with eng.Fori(1, PAIRS) as j:
        body(2 * j, 0, j)
        body(2 * j + 1, 1, j)


def build(nc, x, wqT, bq, wvT, bv, wconv, forward, inverse, consts, out):
    ctx = ExitStack()
    with ctx:
        def sb(name, shape, dt=F32):
            return ctx.enter_context(nc.sbuf_tensor(name, shape, dt))

        def sem(name):
            return ctx.enter_context(nc.semaphore(name))

        value = sb("value", [P, HALVES, PIX])
        rstd = sb("rstd", [P, 2, HALVES])
        nbias = sb("nbias", [P, 2, HALVES])
        zeros = sb("zeros", [P, HALVES, W])

        front = ExitStack()

        def fb(name, shape, dt=F32):
            return front.enter_context(nc.sbuf_tensor(name, shape, dt))

        with nc.sbuf_tensor("xn", [P, HALVES, PIX], F32) as xn:
            pass
        u_w = sb("u_w", [P, NK, POS, 2, C], F32R)
        region_w = fb("region_w", [P, NK * 3 * C + 2 * MODS * TILES])
        fwd_words = TILES * SK // 2
        fwd_u16 = region_w[:, 0:fwd_words].bitcast(U16)
        fwd_sb = region_w[:, 0:fwd_words].bitcast(BF16)
        raw = region_w[:, 0:NK * 3 * C].rearrange("p (n r o) -> p n r o", n=NK, r=3)
        qmax = region_w[:, NK * 3 * C:NK * 3 * C + MODS * TILES]
        mask_px = region_w[:, NK * 3 * C + MODS * TILES:]
        bq_rows = region_w[:, fwd_words:fwd_words + C]
        bq_rest = region_w[:, fwd_words + C:fwd_words + 2 * C]
        sums_sb = region_w[:, fwd_words + 2 * C:fwd_words + 3 * C]
        scratch = fb("scratch", [P, 5632])
        level = scratch[:, 0:2048].rearrange("p (s a n) -> p s a n", s=2, a=HALVES)
        nearest = scratch[:, 2048:3072].bitcast(BF16).rearrange("p (s a n) -> p s a n", s=2, a=HALVES)
        whole = scratch[:, 3072:4096].bitcast(BF16).rearrange("p (s a n) -> p s a n", s=2, a=HALVES)
        qT = scratch[:, 4096:5120].bitcast(BF16).rearrange("p (s t c) -> p s t c", s=2, t=CT)
        wv_sb = scratch[:, 5120:5632].rearrange("p (a o) -> p a o", a=HALVES)
        table_ring = fb("table_ring", [SK, 2, 2, CHUNK], F32R)
        sq_re = scratch[:, 0:1024]
        sq_im = scratch[:, 1024:2048]
        fq = scratch[:, 2048:4096].rearrange("p (u a n) -> p u a n", u=2, a=HALVES)
        w_tmp = fb("w_tmp", [P, 3, C])
        x_ring = scratch[:, 0:2048].rearrange("p (u a n) -> p u a n", u=2, a=HALVES)
        mask_rep = scratch[:, 2048:3072].rearrange("p (u t g k) -> p u t g k", u=2, t=CT, k=MODS)
        wq_sb = fb("wq_sb", [P, HALVES, C])
        cst = fb("cst", [P, 2 * P + SK])
        ident, group_mean, stacker = cst[:, 0:P], cst[:, P:2 * P], cst[0:SK, 2 * P:2 * P + SK]
        ident_b = fb("ident_b", [P, P], BF16)
        ones_b = fb("ones_b", [SK, P], BF16)
        bq_parts = fb("bq_parts", [SK, C], BF16)
        bq_cast = fb("bq_cast", [SK, C], BF16)
        stacked = fb("stacked", [SK, C], F32R)
        bv_sb = fb("bv_sb", [P, HALVES])
        stats = fb("stats", [P, HALVES, CHUNKS, 6])
        mv = fb("mv", [P, HALVES, 2])
        gn_t = fb("gn_t", [P, 8, HALVES])
        ext = fb("ext", [P, 2, LOADS])
        qz = fb("qz", [P, 6, HALVES])

        front.close()
        v_ring = sb("v_ring", [P, VS, 2, TR, HALVES, W + 2], F32R)
        xc = sb("xc", [P, XR, HALVES, W])
        t_buf = sb("t_buf", [P, 2, TR, HALVES * W])
        v_buf = sb("v_buf", [P, 2, TR, HALVES * W])
        odd_b = sb("odd_b", [P, HALVES, TR, W])
        sum_b = sb("sum_b", [P, HALVES, TR, W])

        psum = ctx.enter_context(nc.psum_tensor("psum", [P, 8, CHUNK], F32))
        qT_ps = psum[:, 0:2].rearrange("p s n -> p (s n)").bitcast(BF16).rearrange(
            "p (s t c) -> p s t c", s=2, t=CT)
        v_ps = psum[:, 4:6]
        sums_ps = psum[:, 6]
        small_ps = psum[:, 7]
        field_ps = psum[:, 0:4].rearrange("p (f a) n -> p f a n", f=2)
        query_ps = psum[:, 4:8]
        mask_ps = [psum[:, 0], psum[:, 1]]

        s_x = [[sem(f"x_in{a}_{i}") for i in range(LOADS)] for a in range(HALVES)]
        s_cst, s_wv, s_bias, s_fwd, s_wq = (sem(n) for n in (
            "cst_in", "wv_in", "bias_in", "fwd_in", "wq_in"))
        s_table = [sem("table_in0"), sem("table_in1")]
        s_xr = [sem("x_again0"), sem("x_again1")]
        dve_step = sem("dve_step")
        s_prep = sem("prep_done")
        s_ident = sem("bf16_identities")
        s_gps = sem("group_psum")
        s_gin = sem("group_in")
        s_var = sem("variance_ready")
        s_std = sem("std_ready")
        s_norm = sem("norm_ready")
        s_xn = sem("xn_ready")
        s_ext = sem("extrema_ready")
        s_qz = sem("level_scale_ready")
        s_abs, s_level, s_near, s_quant = (sem(n) for n in (
            "abs_ready", "level_ready", "nearest_ready", "quantised"))
        s_T, s_qT, s_dft = sem("transposed"), sem("qT_ready"), sem("sums_added")
        s_v, s_vout = sem("v_product"), sem("v_ready")
        s_ssb, s_stack_ps, s_stack = (sem(n) for n in ("sums_copied", "sums_stacked_psum", "sums_stacked"))
        s_field, s_sq, s_pow, s_fq = (sem(n) for n in (
            "field_ready", "squares_ready", "power_ready", "fq_ready"))
        s_query, s_qmax = sem("query_ready"), sem("query_reduced")
        s_mask, s_rep, s_mT = sem("mask_ready"), sem("mask_spread"), sem("mask_transposed")
        s_gain, s_x1, s_stat2 = sem("gained"), sem("x1_ready"), sem("x1_counted")
        s_raw, s_wstep = sem("raw_in"), sem("weight_step")
        s_above = sem("above_ready")
        s_zero, s_halo, s_xc = sem("zeros_ready"), sem("halo_ready"), sem("chunk_rows_ready")
        s_t, s_vt, s_hi, s_lo = (sem(n) for n in ("transform_step", "transformed", "hi_ready", "lo_ready"))
        s_m, s_e, s_sd, s_y = (sem(n) for n in ("product_ready", "product_copied", "sum_diff_ready", "rows_added"))
        s_stored = sem("out_stored")

        block = ctx.enter_context(nc.Block())

        def chunk(i, u):
            return bass.ds((2 * i + u) * CHUNK, CHUNK)

        def pair(i):
            return bass.ds(2 * i * CHUNK, 2 * CHUNK)

        def transformed(p):
            return v_buf[:, p % 2].rearrange("p t (k w) -> p (t k) w", w=W)

        def split_part(p, part):
            return v_ring[:, p % VS, part, :, :, 1:W + 1].rearrange("p t k w -> p (t k) w")

        def product(p, m):
            return psum[:, (HALVES * p + m) % 6, 0:TR * W].rearrange("p (t w) -> p t w", w=W)

        @block.sync
        def _(sp):
            for a in range(HALVES):
                for i in range(LOADS):
                    sp.dma_start(xn[:, a, i * LOADW:(i + 1) * LOADW],
                                 x[a * P:(a + 1) * P, i * LOADW:(i + 1) * LOADW]).then_inc(s_x[a][i], 16)
                if a == 0:
                    sp.dma_start(cst[:, :], consts).then_inc(s_cst, 16)
            sp.dma_start(fwd_u16, forward.rearrange("p t k -> p (t k)")).then_inc(s_fwd, 16)
            sp.dma_start(wv_sb, wvT.rearrange("(a p) o -> p a o", p=P)).then_inc(s_wv, 16)
            sp.dma_start(wq_sb[:, :, :], wqT.rearrange("(a p) o -> p a o", p=P)).then_inc(s_wq, 16)
            sp.dma_start(bv_sb[:, :], bv).then_inc(s_bias, 16)
            sp.wait_ge(s_prep, 3)
            for r in range(3):
                sp.dma_start(bq_rows[r * SBLK:r * SBLK + 1, :], bq.rearrange("(a n) -> a n", a=1)
                             ).then_inc(s_bias, 16)

            sp.wait_ge(s_dft, CHUNKS)
            sp.wait_ge(s_stack_ps, 1)
            sp.dma_start(region_w[:, 0:NK * 3 * C].rearrange("p (a n) -> p a n", a=HALVES),
                         wconv.rearrange("(a p) n -> p a n", p=P)).then_inc(s_raw, 16)

            def x_again(i, first):
                for u in range(2):
                    if not first:
                        sp.wait_ge(s_x1, 4 * i + 2 * u - 2)
                    sp.dma_start(x_ring[:, u], x.rearrange("(a p) n -> p a n", p=P)[:, :, chunk(i, u)]
                                 ).then_inc(s_xr[u], 16)

            sp.wait_ge(s_fq, CHUNKS)
            peeled(sp, PAIRS, x_again)
            with sp.Fori(0, CCH) as i:
                sp.wait_ge(s_y, YS * i + YS)
                sp.dma_start(out.rearrange("(a p) n -> p a n", p=P)[:, :, bass.ds(i * CW, CW)],
                             value[:, :, bass.ds(i * CW, CW)]).then_inc(s_stored, 16)
            sp.wait_ge(s_stored, 16 * CCH)

        @block.gpsimd
        def _(pool):
            pool.memset(bq_rows[0:SK, :], 0.0).then_inc(s_prep, 1)
            pool.memset(ones_b[:, :], 1.0).then_inc(s_prep, 1)
            pool.memset(bq_parts[:, :], 0.0).then_inc(s_prep, 1)
            pool.memset(zeros[:, :, :], 0.0).then_inc(s_zero, 1)

            def table(i, first):
                for u in range(2):
                    if not first:
                        pool.wait_ge(s_field, 2 * i + u - 1)

                    pool.dma_start(table_ring[:, u], inverse[:, bass.ds(2 * i + u, 1)].rearrange(
                        "k o f n -> k (o f) n")).then_inc(s_table[u], 16)

            peeled(pool, PAIRS, table)
            with pool.Fori(0, PAIRS) as i:
                for u in range(2):
                    pool.wait_ge(s_xr[u], 16 * (i + 1))
                    for a in range(HALVES):
                        pool.wait_ge(s_gain, 4 * i + 2 * u + a + 1)
                        v = value[:, a, chunk(i, u)]
                        pool.tensor_tensor(v, v, x_ring[:, u, a], ALU.add).then_inc(s_x1, 1)
            pool.wait_ge(s_norm, 3)
            for col in (0, W + 1):
                pool.memset(v_ring[:, :, :, :, :, col:col + 1].rearrange("p s l t k c -> p (s l t k) c").bitcast(F32), 0.0
                            ).then_inc(s_zero, 1)

        @block.scalar
        def _(act):
            def std(n, lo, hi):
                act.wait_ge(s_var, n)
                act.activation(gn_t[:, 4, lo:hi], gn_t[:, 3, lo:hi], ACT.Sqrt).then_inc(s_std, 1)

            def normalise(a):
                act.wait_ge(s_norm, a + 1)
                with act.Fori(0, LOADS) as c:
                    v = xn[:, a, bass.ds(c * LOADW, LOADW)]
                    act.activation(v, v, ACT.Identity, bias=nbias[:, 0, a:a + 1],
                                   scale=rstd[:, 0, a:a + 1]).then_inc(s_xn, 1)

            def levels(c, slot, j):
                if not isinstance(c, int):
                    act.wait_ge(s_quant, c - 1)
                act.activation(level[:, slot], xn[:, :, bass.ds(c * CHUNK, CHUNK)], ACT.Abs).then_inc(s_abs, 1)
                act.wait_ge(s_abs, c + 1)
                for a in range(HALVES):
                    act.activation(level[:, slot, a], level[:, slot, a], ACT.Relu, bias=qz[:, 4, a:a + 1],
                                   scale=qz[:, 3, a:a + 1]).then_inc(s_level, 1)
                if slot == 0 and not isinstance(c, int):
                    v_copy(j + (VLEAD - 1))

            def v_copy(c):
                for m in range(HALVES):
                    act.wait_ge(s_v, 2 * c + m + 1)
                    act.activation(value[:, m, bass.ds(c * CHUNK, CHUNK)], v_ps[:, m],
                                   ACT.Identity, bias=bv_sb[:, m:m + 1]).then_inc(s_vout, 1)

            std(1, 0, 1)
            normalise(0)
            std(2, 1, 2)
            normalise(1)
            act.wait_ge(s_bias, 16 * 4)
            with act.Fori(0, VLEAD) as c:
                v_copy(c)
            act.wait_ge(s_qz, 2)
            alternating(act, levels)
            v_copy(CHUNKS - 1)

            def modulus(i, first):
                for u in range(2):
                    c = 2 * i + u
                    act.wait_ge(s_field, c + 1)
                    if not (first and u == 0):
                        act.wait_ge(s_pow, c)
                    act.activation(sq_im, field_ps[:, 1].rearrange("p a n -> p (a n)"), ACT.Square
                                   ).then_inc(s_sq, 1)
                    if not (first and u == 0):
                        act.wait_ge(s_fq, c)
                    act.activation(sq_re, field_ps[:, 0].rearrange("p a n -> p (a n)"), ACT.Square
                                   ).then_inc(s_sq, 1)
                    act.wait_ge(s_pow, c + 1)
                    if not first:
                        act.wait_ge(s_query, c - 1)
                    act.activation(fq[:, u].rearrange("p a n -> p (a n)"), sq_re, ACT.Sqrt).then_inc(s_fq, 1)

            peeled(act, PAIRS, modulus)

            def spread(i, first):
                for u in range(2):
                    if not first:
                        act.wait_ge(s_mT, 2 * i + u - 1)
                    src = mask_px[:, bass.ds((2 * i + u) * CT * MODS, CT * MODS)].rearrange(
                        "p (t g k) -> p t g k", t=CT, g=1).broadcast_to([P, CT, P // MODS, MODS])
                    act.activation(mask_rep[:, u], src, ACT.Copy).then_inc(s_rep, 1)

            act.wait_ge(s_mask, 1)
            peeled(act, PAIRS, spread)
            std(3, 0, 2)
            act.wait_ge(s_norm, 3)
            act.wait_ge(s_zero, 3)

            def rows(c, lo, n):
                for k in range(HALVES):
                    src = value[:, k, bass.ds(c * CW + (lo - 1) * W, n * W)]
                    act.activation(xc[:, lo:lo + n, k, :], src.rearrange("p (h w) -> p h w", w=W), ACT.Identity,
                                   bias=nbias[:, 1, k:k + 1], scale=rstd[:, 1, k:k + 1]).then_inc(s_xc, 1)

            def next_rows(c, last=False):
                act.wait_ge(s_vt, POS * c)
                act.activation(xc[:, 0:2], xc[:, CR:XR], ACT.Copy).then_inc(s_halo, 1)
                act.wait_ge(s_halo, c + 1)
                if last:
                    act.activation(xc[:, XR - 1], zeros[:, :, :], ACT.Copy).then_inc(s_halo, 1)
                rows(c, 2, CR - 1 if last else CR)

            def hi(c, p, first=False):
                q = POS * c + p
                act.wait_ge(s_vt, q + 1)
                if not (first and p < VS):
                    act.wait_ge(s_m, 2 * q - 2 * VS + 2)
                act.activation(split_part(p, 0), transformed(p), ACT.Copy).then_inc(s_hi, 1)

            def copy_product(i, p, first):
                for m in range(HALVES):
                    act.wait_ge(s_m, 2 * (POS * i + p) + m + 1)
                    if p == 3 or not first:
                        act.wait_ge(s_y, YS * i + (8 if p == 3 else 0))
                    act.activation(odd_b[:, m], product(p, m), ACT.Copy).then_inc(s_e, 1)

            def conv_copies(i, first=False, before_last=False, last=False):
                for p in range(POS):
                    if p in (2, 4):
                        copy_product(i, p - 1, first)
                    if p < POS - 2:
                        hi(i, p + 2, first)
                    elif not last:
                        hi(i + 1, p + 2 - POS)
                    if p == 2 and not last:
                        next_rows(i + 1, before_last)

            act.activation(xc[:, 0], zeros[:, :, :], ACT.Copy).then_inc(s_halo, 1)
            rows(0, 1, XR - 1)
            hi(0, 0, True)
            hi(0, 1, True)
            conv_copies(0, first=True)
            with act.Fori(1, CCH - 2) as i:
                conv_copies(i)
            conv_copies(CCH - 2, before_last=True)
            conv_copies(CCH - 1, last=True)

        @block.tensor
        def _(pe):
            def group_sums(n, lo, hi):
                pe.wait_ge(s_gin, 2 * n + 1)
                pe.matmul(small_ps[:, 8 * n:8 * n + hi - lo], group_mean, mv[:, lo:hi, 0],
                          start=True, stop=True).then_inc(s_gps, 1)
                pe.wait_ge(s_gin, 2 * n + 2)
                pe.matmul(small_ps[:, 8 * n + 4:8 * n + 4 + hi - lo], group_mean, gn_t[:, 2, lo:hi],
                          start=True, stop=True).then_inc(s_gps, 1)

            def transposes(c, slot, j):
                pe.wait_ge(s_quant, c + 1)
                if not isinstance(c, int):
                    pe.wait_ge(s_qT, c - 1)
                for t in range(CT):
                    for a in range(HALVES):
                        last = pe.transpose(qT_ps[:, slot, t, a * P:(a + 1) * P],
                                            whole[:, slot, a, t * P:(t + 1) * P], ident_b[:, :])
                last.then_inc(s_T, 1)
                if slot == 0:
                    v_product(j + VLEAD, False)
                if not (isinstance(c, int) and c == 0):
                    sums(c - 1, 1 - slot, start=isinstance(c, int))

            def sums(c, slot, start=False, stop=False):
                pe.wait_ge(s_qT, c + 1)
                for t in range(CT):
                    last = pe.matmul(sums_ps[0:SK, 0:C], fwd_sb[:, bass.ds((c * CT + t) * SK, SK)],
                                     qT[:, slot, t], start=start and t == 0, stop=stop and t == CT - 1)
                last.then_inc(s_dft, 1)

            def v_product(c, first):
                for m in range(HALVES):
                    if not first:
                        pe.wait_ge(s_vout, 2 * c + m - 1)
                    for k in range(HALVES):
                        last = pe.matmul(v_ps[:, m], wv_sb[:, k, m * P:(m + 1) * P],
                                         xn[:, k, bass.ds(c * CHUNK, CHUNK)], start=k == 0, stop=k == HALVES - 1)
                    last.then_inc(s_v, 1)

            pe.wait_ge(s_cst, 16)
            group_sums(0, 0, 1)
            group_sums(1, 1, 2)
            pe.wait_ge(s_ident, 1)
            pe.wait_ge(s_fwd, 16)
            pe.wait_ge(s_wv, 16)
            pe.wait_ge(s_xn, 2 * LOADS)
            v_product(0, True)
            with pe.Fori(1, VLEAD) as c:
                v_product(c, False)
            alternating(pe, transposes)
            sums(CHUNKS - 1, 1, stop=True)
            pe.wait_ge(s_ssb, 1)
            pe.matmul(small_ps[0:SK, 0:C], stacker, sums_sb[0:SK, :], start=True, stop=True).then_inc(s_stack_ps, 1)

            def fields(i, u, first):
                pe.wait_ge(s_table[u], 16 * (i + 1))
                for part in (1, 0):
                    if not first:
                        pe.wait_ge(s_sq, 4 * i + 2 * u - part)
                    for a in range(HALVES):
                        last = pe.matmul(field_ps[:, part, a], stacked[:, a * P:(a + 1) * P],
                                         table_ring[:, u, part], start=True, stop=True)
                last.then_inc(s_field, 1)

            def query(i, u, first):
                pe.wait_ge(s_fq, 2 * i + u + 1)
                if not first:
                    pe.wait_ge(s_qmax, 2 * i + u - 1)
                for t in range(CT):
                    o = query_ps[:, 2 * u + t // 2, (t % 2) * C:(t % 2 + 1) * C]
                    for a in range(HALVES):
                        pe.matmul(o, fq[:, u, a, t * P:(t + 1) * P], wq_sb[:, a, :], start=a == 0, stop=False)
                    last = pe.matmul(o, ones_b[:, :], bq_parts[:, :], start=False, stop=True)
                last.then_inc(s_query, 1)

            pe.wait_ge(s_stack, 1)
            pe.wait_ge(s_wq, 16)
            pe.wait_ge(s_vout, 2 * CHUNKS)
            fields(0, 0, True)
            fields(0, 1, False)
            query(0, 0, True)
            fields(1, 0, False)
            query(0, 1, True)
            with pe.Fori(1, PAIRS - 1) as i:
                fields(i, 1, False)
                query(i, 0, False)
                fields(i + 1, 0, False)
                query(i, 1, False)
            fields(PAIRS - 1, 1, False)
            query(PAIRS - 1, 0, False)
            query(PAIRS - 1, 1, False)

            def mask_transposes(i, first):
                for u in range(2):
                    pe.wait_ge(s_rep, 2 * i + u + 1)
                    if not first:
                        pe.wait_ge(s_gain, 4 * i + 2 * u - 2)
                    for t in range(CT):
                        last = pe.transpose(mask_ps[u][:, t * P:(t + 1) * P],
                                            mask_rep[:, u, t].rearrange("p g k -> p (g k)"), ident)
                    last.then_inc(s_mT, 1)

            peeled(pe, PAIRS, mask_transposes)
            group_sums(2, 0, 2)

            def conv(i, first):
                for p in range(POS):
                    pe.wait_ge(s_lo, POS * i + p + 1)
                    for m in range(HALVES):
                        if p in (3, 5):
                            pe.wait_ge(s_sd, 8 * i + (3 if p == 3 else 7) + m)
                        elif p == 4:
                            pe.wait_ge(s_e, 4 * i + m + 1)
                        elif p == 0 and not first:
                            pe.wait_ge(s_e, 4 * i - 1 + m)
                        elif not first:
                            pe.wait_ge(s_y, YS * i - (3 if p == 1 else 1) + m)
                        for n in range(NK):
                            for j, (wl, vl) in enumerate(((0, 0), (0, 1), (1, 0))):
                                last = pe.matmul(product(p, m).rearrange("p t w -> p (t w)"),
                                                 u_w[:, n, p, wl, m * P:(m + 1) * P],
                                                 v_ring[:, p % VS, vl, :, n // 3, n % 3:n % 3 + W],
                                                 start=n == 0 and j == 0, stop=n == NK - 1 and j == 2)
                        last.then_inc(s_m, 1)

            peeled(pe, CCH, conv)

        @block.vector
        def _(dve):
            steps = [0]

            def step(ins):
                steps[0] += 1
                ins.then_inc(dve_step, 1)
                dve.wait_ge(dve_step, steps[0])

            def group_norm(layer, n, lo, hi):
                w = hi - lo
                row = [gn_t[:, j, lo:hi] for j in range(8)]
                for a in range(lo, hi):
                    ins = dve.bn_aggr(mv[:, a, :], stats[:, a].rearrange("p c s -> p (c s)"))
                ins.then_inc(s_gin, 1)
                dve.wait_ge(s_gin, 2 * n + 1)
                dve.wait_ge(s_gps, 2 * n + 1)
                mean = small_ps[:, 8 * n:8 * n + w]
                step(dve.tensor_tensor(row[0], mv[:, lo:hi, 0], mean, ALU.subtract))
                step(dve.tensor_copy(row[1], mean))
                step(dve.tensor_tensor(row[2], row[0], row[0], ALU.mult))
                dve.tensor_tensor(row[2], row[2], mv[:, lo:hi, 1], ALU.add).then_inc(s_gin, 1)
                dve.wait_ge(s_gps, 2 * n + 2)
                dve.tensor_scalar(row[3], small_ps[:, 8 * n + 4:8 * n + 4 + w], EPS, None, ALU.add
                                  ).then_inc(s_var, 1)
                dve.wait_ge(s_std, n + 1)
                dve.wait_ge(s_var, n + 1)
                step(dve.reciprocal(row[5], row[4]))
                step(dve.tensor_tensor(row[6], row[5], row[5], ALU.mult))
                step(dve.tensor_tensor(row[6], row[6], row[3], ALU.mult))
                step(dve.tensor_scalar(row[6], row[6], -0.5, 1.5, ALU.mult, ALU.add))
                step(dve.tensor_tensor(rstd[:, layer, lo:hi], row[5], row[6], ALU.mult))
                dve.scalar_tensor_tensor(nbias[:, layer, lo:hi], row[1], -1.0, rstd[:, layer, lo:hi],
                                         ALU.mult, ALU.mult).then_inc(s_norm, 1)

            def half_stats(a):
                for i in range(LOADS):
                    dve.wait_ge(s_x[a][i], 16)
                    for j in range(LOADW // CHUNK):
                        ins = dve.bn_stats(stats[:, a, i * (LOADW // CHUNK) + j],
                                           xn[:, a, i * LOADW + j * CHUNK:i * LOADW + (j + 1) * CHUNK])
                step(ins)

            def extrema(a):
                with dve.Fori(0, LOADS) as c:
                    dve.wait_ge(s_xn, c + (1 + a * LOADS))
                    for j, op in enumerate((ALU.max, ALU.min)):
                        dve.tensor_reduce(ext[:, j, bass.ds(c, 1)], xn[:, a, bass.ds(c * LOADW, LOADW)], AX.X, op,
                                          apply_absolute_value=True).then_inc(s_ext, 1)
                dve.wait_ge(s_ext, 2 * LOADS * (a + 1))
                z = [qz[:, j, a:a + 1] for j in range(6)]
                step(dve.tensor_reduce(z[0], ext[:, 0, 0:LOADS], AX.X, ALU.max))
                step(dve.tensor_reduce(z[1], ext[:, 1, 0:LOADS], AX.X, ALU.min))
                step(dve.tensor_tensor(z[2], z[0], z[1], ALU.subtract))
                step(dve.reciprocal(z[5], z[2]))
                step(dve.tensor_scalar(z[3], z[5], 255.0 * (1.0 + 2.0 ** -22), None, ALU.mult))
                dve.scalar_tensor_tensor(z[4], z[1], -1.0, z[3], ALU.mult, ALU.mult).then_inc(s_qz, 1)

            def flat(t):
                return t.rearrange("p a n -> p (a n)")

            def quantise(c, slot, j):
                dve.wait_ge(s_level, 2 * c + 2)
                if not isinstance(c, int):
                    dve.wait_ge(s_T, c - 1)
                near, out_ = flat(nearest[:, slot]), flat(whole[:, slot])
                dve.tensor_scalar(near, flat(level[:, slot]), ROUND, -ROUND, ALU.add, ALU.add).then_inc(s_near, 1)
                dve.wait_ge(s_near, c + 1)
                dve.tensor_tensor(out_, flat(level[:, slot]), near, ALU.is_lt).then_inc(s_above, 1)
                if not (isinstance(c, int) and c == 0):
                    copy_tiles(c - 1, 1 - slot)
                dve.wait_ge(s_above, c + 1)
                dve.tensor_tensor(out_, near, out_, ALU.subtract).then_inc(s_quant, 1)

            def copy_tiles(c, slot):
                dve.wait_ge(s_T, c + 1)
                if not isinstance(c, int) or c > 1:
                    dve.wait_ge(s_dft, c - 1)
                dve.tensor_copy(qT[:, slot], qT_ps[:, slot]).then_inc(s_qT, 1)

            half_stats(0)
            group_norm(0, 0, 0, 1)
            half_stats(1)
            group_norm(0, 1, 1, 2)
            dve.tensor_copy(ident_b[:, :], ident).then_inc(s_ident, 1)
            extrema(0)
            extrema(1)
            alternating(dve, quantise)
            copy_tiles(CHUNKS - 1, 1)

            dve.wait_ge(s_bias, 16 * 4)
            for part in range(3):
                rows = slice(part * SBLK, part * SBLK + 1)
                src = bq_rows if part == 0 else bq_rest
                step(dve.tensor_copy(bq_cast[:, :], src[0:SK, :]))
                step(dve.tensor_copy(bq_parts[rows, :], bq_cast[rows, :]))
                if part < 2:
                    step(dve.tensor_tensor(bq_rest[0:SK, :], src[0:SK, :], bq_cast[:, :], ALU.subtract))

            dve.wait_ge(s_dft, CHUNKS)
            dve.tensor_copy(sums_sb[0:SK, :], sums_ps[0:SK, 0:C]).then_inc(s_ssb, 1)
            dve.wait_ge(s_stack_ps, 1)
            step(dve.tensor_copy(stacked[:, :], small_ps[0:SK, 0:C]))
            lo = slice(2 * SBLK, SK)
            dve.tensor_tensor(stacked[lo, :], small_ps[lo, 0:C], stacked[lo, :].bitcast(F32), ALU.subtract
                              ).then_inc(s_stack, 1)

            def power(c):
                dve.wait_ge(s_sq, 2 * c + 2)
                dve.tensor_tensor(sq_re, sq_re, sq_im, ALU.add).then_inc(s_pow, 1)

            wa, wb, wd = w_tmp[:, 0], w_tmp[:, 1], w_tmp[:, 2]
            STEPS = 18

            def weights(n, part):
                def g(r):
                    return raw[:, bass.ds(n, 1), r].rearrange("p o c -> p (o c)")

                def u(p, l):
                    return u_w[:, bass.ds(n, 1), p, l].rearrange("p o c -> p (o c)")

                def rest(p, exact):
                    return dve.tensor_tensor(u(p, 1), exact, u(p, 0).bitcast(F32), ALU.subtract)

                def after(k):
                    dve.wait_ge(s_wstep, n * STEPS + k)

                def last_unit():
                    if not (isinstance(n, int) and n == 0):
                        dve.wait_ge(s_wstep, n * STEPS)

                if part == 0:
                    last_unit()
                    dve.tensor_tensor(wa, g(0), g(2), ALU.add).then_inc(s_wstep, 1)
                    dve.scalar_tensor_tensor(wb, g(2), 4.0, g(0), ALU.mult, ALU.add).then_inc(s_wstep, 1)
                    dve.tensor_copy(u(4, 0), g(0)).then_inc(s_wstep, 1)
                    dve.tensor_copy(u(5, 0), g(2)).then_inc(s_wstep, 1)
                elif part == 1:
                    after(1)
                    dve.tensor_tensor(wd, wa, g(1), ALU.add).then_inc(s_wstep, 1)
                    after(4)
                    rest(4, g(0)).then_inc(s_wstep, 1)
                    rest(5, g(2)).then_inc(s_wstep, 1)
                    after(5)
                    dve.tensor_tensor(wa, wa, g(1), ALU.subtract).then_inc(s_wstep, 1)
                    dve.tensor_copy(u(0, 0), wd).then_inc(s_wstep, 1)
                elif part == 2:
                    after(8)
                    dve.tensor_copy(u(1, 0), wa).then_inc(s_wstep, 1)
                    after(9)
                    rest(0, wd).then_inc(s_wstep, 1)
                    after(10)
                    rest(1, wa).then_inc(s_wstep, 1)
                    after(11)
                    dve.scalar_tensor_tensor(wd, g(1), 2.0, wb, ALU.mult, ALU.add).then_inc(s_wstep, 1)
                    after(13)
                    dve.scalar_tensor_tensor(wb, g(1), -2.0, wb, ALU.mult, ALU.add).then_inc(s_wstep, 1)
                else:
                    after(13)
                    dve.tensor_copy(u(2, 0), wd).then_inc(s_wstep, 1)
                    after(14)
                    dve.tensor_copy(u(3, 0), wb).then_inc(s_wstep, 1)
                    after(15)
                    rest(2, wd).then_inc(s_wstep, 1)
                    after(16)
                    rest(3, wb).then_inc(s_wstep, 1)

            def query_max(i, u):
                dve.wait_ge(s_query, 2 * i + u + 1)
                src = query_ps[:, 2 * u:2 * u + 2, :].rearrange("p b (t c k) -> p k (b t) c", t=2, k=MODS)
                dst = qmax.rearrange("p (k t) -> p k t", k=MODS)[:, :, bass.ds((2 * i + u) * CT, CT)]
                dve.tensor_reduce(dst, src, AX.X, ALU.max).then_inc(s_qmax, 1)

            def query_pair(i, unit=None):
                for u in range(2):
                    power(2 * i + u + 1)
                    if unit is not None:
                        weights(unit, 2 * u)
                    query_max(i, u)
                    if unit is not None:
                        weights(unit, 2 * u + 1)

            power(0)
            dve.wait_ge(s_raw, 16)
            query_pair(0, 0)
            with dve.Fori(1, NK) as i:
                query_pair(i, i)
            with dve.Fori(NK, PAIRS - 1) as i:
                query_pair(i)
            power(2 * PAIRS - 1)
            query_max(PAIRS - 1, 0)
            query_max(PAIRS - 1, 1)
            dve.wait_ge(s_qmax, CHUNKS)
            for r in range(1, MODS * TILES // QCOLS):
                step(dve.tensor_tensor(qmax[:, 0:QCOLS], qmax[:, 0:QCOLS], qmax[:, r * QCOLS:(r + 1) * QCOLS],
                                       ALU.max))
            by_tile = mask_px.rearrange("p (t k) -> p k t", k=MODS)
            for k in range(MODS):
                t = 0
                while t < TILES:
                    col = (TILES * k + t) % QCOLS
                    n = min(TILES - t, QCOLS - col)
                    ins = dve.tensor_copy(by_tile[:, k, t:t + n], qmax[:, col:col + n])
                    t += n
            ins.then_inc(s_mask, 1)

            def gain(i, u, a):
                v = value[:, a, chunk(i, u)]
                dve.scalar_tensor_tensor(v, mask_ps[u][:, :], 1.0, v, ALU.add, ALU.mult).then_inc(s_gain, 1)

            def x1_stats(i, u):
                for a in range(HALVES):
                    dve.wait_ge(s_x1, 4 * i + 2 * u + a + 1)
                    dve.bn_stats(stats[:, a, bass.ds(2 * i + u, 1)].rearrange("p o s -> p (o s)"),
                                 value[:, a, chunk(i, u)]).then_inc(s_stat2, 1)

            def gains(i, u):
                dve.wait_ge(s_mT, 2 * i + u + 1)
                for a in range(HALVES):
                    gain(i, u, a)

            gains(0, 0)
            with dve.Fori(0, PAIRS - 1) as i:
                gains(i, 1)
                x1_stats(i, 0)
                gains(i + 1, 0)
                x1_stats(i, 1)
            gains(PAIRS - 1, 1)
            x1_stats(PAIRS - 1, 0)
            x1_stats(PAIRS - 1, 1)
            dve.wait_ge(s_stat2, 2 * CHUNKS)
            group_norm(1, 2, 0, 2)

            def transform(c, p):
                d = [xc[:, j:j + WT * (TR - 1) + 1:WT].rearrange("p t k w -> p t (k w)") for j in range(6)]
                v, t1, t2 = v_buf[:, p % 2], t_buf[:, 0], t_buf[:, 1]
                steps = (2, 2, 4, 4, 5, 6)[p]
                first = isinstance(c, int) and c == 0
                if p == 0:
                    dve.wait_ge(s_xc, 2 * c + 2)
                if p in (0, 2, 4, 5) and not (first and p == 0):
                    dve.wait_ge(s_vt, POS * c + p)
                if p == 0:
                    dve.scalar_tensor_tensor(t1, d[2], -4.0, d[4], ALU.mult, ALU.add).then_inc(s_t, 1)
                    dve.scalar_tensor_tensor(t2, d[1], -4.0, d[3], ALU.mult, ALU.add).then_inc(s_t, 1)
                elif p == 2:
                    dve.tensor_tensor(t1, d[4], d[2], ALU.subtract).then_inc(s_t, 1)
                    dve.tensor_tensor(t2, d[3], d[1], ALU.subtract).then_inc(s_t, 1)
                elif p == 4:
                    dve.scalar_tensor_tensor(t1, d[2], -5.0, d[4], ALU.mult, ALU.add).then_inc(s_t, 1)
                elif p == 5:
                    dve.scalar_tensor_tensor(t2, d[3], -5.0, d[5], ALU.mult, ALU.add).then_inc(s_t, 1)
                dve.wait_ge(s_t, POS * c + steps)
                if not (first and p < 2):
                    dve.wait_ge(s_lo, POS * c + p - 1)
                if p == 0:
                    ins = dve.tensor_tensor(v, t1, t2, ALU.add)
                elif p == 1:
                    ins = dve.tensor_tensor(v, t1, t2, ALU.subtract)
                elif p in (2, 3):
                    ins = dve.scalar_tensor_tensor(v, t2, 2.0 if p == 2 else -2.0, t1, ALU.mult, ALU.add)
                else:
                    ins = dve.scalar_tensor_tensor(v, d[p - 4], 4.0, t1 if p == 4 else t2, ALU.mult, ALU.add)
                ins.then_inc(s_vt, 1)

            def split(c, p):
                dve.wait_ge(s_hi, POS * c + p + 1)
                dve.tensor_tensor(split_part(p, 1), transformed(p), split_part(p, 0).bitcast(F32), ALU.subtract
                                  ).then_inc(s_lo, 1)

            def out_rows(i, m, j, n=1):
                v = value[:, m, bass.ds(i * CW, CW)].rearrange("p (t j w) -> p j t w", j=WT, w=W)
                return v[:, j:j + 2 * n - 1:2]

            def add(i, m, j, term, factor):
                dst = out_rows(i, m, j).rearrange("p j t w -> p (j t) w")
                dve.scalar_tensor_tensor(dst, term, factor, dst, ALU.mult, ALU.add).then_inc(s_y, 1)

            def take(i, p, first=False):
                if p in (1, 3):
                    base = 8 * i + (0 if p == 1 else 4)
                    for m in range(HALVES):
                        dve.wait_ge(s_e, 4 * i + (p - 1) + m + 1)
                        if not (first and p == 1):
                            dve.wait_ge(s_y, YS * i + (0 if p == 1 else 8))
                        dve.tensor_tensor(sum_b[:, m], product(p - 1, m), odd_b[:, m], ALU.add
                                          ).then_inc(s_sd, 1)
                    for m in range(HALVES):
                        dve.wait_ge(s_sd, base + m + 1)
                        dve.tensor_tensor(odd_b[:, m], product(p - 1, m), odd_b[:, m], ALU.subtract
                                          ).then_inc(s_sd, 1)
                if p == 1:
                    for m in range(HALVES):
                        dve.wait_ge(s_sd, base + m + 3)
                        for j, term in ((0, sum_b), (1, odd_b)):
                            for jj in (j, j + 2):
                                add(i, m, jj, term[:, m], -1.0 / 6.0)
                elif p == 3:
                    for m in range(HALVES):
                        dve.wait_ge(s_sd, base + m + 3)
                        add(i, m, 0, sum_b[:, m], 1.0 / 24.0)
                        add(i, m, 2, sum_b[:, m], 4.0 / 24.0)
                        add(i, m, 1, odd_b[:, m], 2.0 / 24.0)
                        add(i, m, 3, odd_b[:, m], 8.0 / 24.0)
                elif p in (4, 5):
                    for m in range(HALVES):
                        dve.wait_ge(s_m, 2 * (POS * i + p) + m + 1)
                        dve.wait_ge(s_y, YS * i + 16)
                        add(i, m, 0 if p == 4 else 3, product(p, m), 0.25 if p == 4 else 1.0)

            def conv_steps(i, first=False, last=False):
                for p in range(POS):
                    if p < 3:
                        transform(i, p + 3)
                    elif not last:
                        transform(i + 1, p - 3)
                    if p == 0:
                        if not first:
                            take(i - 1, POS - 1)
                    else:
                        take(i, p - 1, first)
                    if p < POS - 2:
                        split(i, p + 2)
                    elif not last:
                        split(i + 1, p + 2 - POS)

            transform(0, 0)
            transform(0, 1)
            split(0, 0)
            transform(0, 2)
            split(0, 1)
            conv_steps(0, first=True)
            with dve.Fori(1, CCH - 1) as i:
                conv_steps(i)
            conv_steps(CCH - 1, last=True)
            take(CCH - 1, POS - 1)


def kernel(x, L0_conv_Wq, L0_conv_bq, L0_conv_Wk, L0_conv_bk, L0_conv_Wv, L0_conv_bv, L1_conv_weight_matrix):
    import concourse.bacc as bacc
    from concourse.bass_utils import run_bass_kernel_spmd

    forward, inverse = frequency_tables()
    arrays = {
        "x": np.ascontiguousarray(np.asarray(x).reshape(C, PIX)),
        "wqT": np.ascontiguousarray(np.asarray(L0_conv_Wq).T),
        "bq": np.asarray(L0_conv_bq),
        "wvT": np.ascontiguousarray(np.asarray(L0_conv_Wv).T),
        "bv": np.ascontiguousarray(np.asarray(L0_conv_bv).reshape(HALVES, P).T),
        "wconv": np.ascontiguousarray(
            np.asarray(L1_conv_weight_matrix).reshape(C, 3, 3, C).transpose(0, 2, 1, 3).reshape(C, 9 * C)),
        "forward": forward,
        "inverse": inverse,
        "consts": small_constants(),
    }
    nc = bacc.Bacc("TRN2", target_bir_lowering=False, num_devices=1)
    aps = {n: nc.dram_tensor(n, a.shape, mybir.dt.from_np(a.dtype), kind="ExternalInput").ap()
           for n, a in arrays.items()}
    out = nc.dram_tensor("out", (C, PIX), F32, kind="ExternalOutput").ap()
    build(nc, **aps, out=out)
    got = run_bass_kernel_spmd(nc, [arrays], core_ids=[0])
    return got.results[0]["out"].reshape(1, C, H, W)
```

```python
from contextlib import ExitStack

import numpy as np

import concourse.bass as bass
from concourse import mybir

ALU = mybir.AluOpType
ACT = mybir.ActivationFunctionType
AX = mybir.AxisListType
F32 = mybir.dt.float32
F32R = mybir.dt.float32r
BF16 = mybir.dt.bfloat16
U16 = mybir.dt.uint16

P = 128
C, H, W = 256, 96, 96
HALVES = C // P
PIX = H * W
TILES = PIX // P
CHUNK = 512
CHUNKS = PIX // CHUNK
CT = CHUNK // P
PAIRS = CHUNKS // 2
VLEAD = CHUNKS - PAIRS - 1
GROUPS = 32
GC = C // GROUPS
MODS = 8
NB = 25
RC = 3 * P
RT = RC // P
RCH = PIX // RC
TRIPLES = MODS
MEMBERS = RCH // TRIPLES
ROUND = 2.0 ** 23
LOADS = 6
LOADW = PIX // LOADS
EXT_FIRST = 4
ACT_LOADS = (1, 2, 3, 4)
EPS = 1e-5
SBLK = 32
SK = 3 * SBLK
NK = 3 * HALVES
POS = 6
WT = 4
CR = 16
TR = CR // WT
CCH = H // CR
CW = CR * W
XR = CR + 2
VS = 3
YS = 20


def frequency_tables():
    def f32r(a):
        b = a.astype(np.float32).view(np.uint32).astype(np.uint64)
        b = (b + 0x7FF + ((b >> 12) & 1)) & 0xFFFFF000
        return b.astype(np.uint32).view(np.float32)

    def bf16_bits(a):
        b = a.astype(np.float32).view(np.uint32).astype(np.uint64)
        return ((b + 0x7FFF + ((b >> 16) & 1)) >> 16).astype(np.uint16)

    def bf16_value(bits):
        return (bits.astype(np.uint32) << 16).view(np.float32).astype(np.float64)

    def basis(n):
        a = 2 * np.pi * np.arange(n) / n
        return np.stack([np.ones(n), np.cos(a), np.sin(a), np.cos(2 * a), np.sin(2 * a)])

    bh, bw = basis(H), basis(W)
    fwd = np.einsum("ih,jw->hwij", bh, bw).reshape(PIX, NB)
    table = np.zeros((PIX, 3, SBLK), np.uint16)
    rest = fwd
    for part in range(3):
        bits = bf16_bits(rest)
        table[:, part, :NB] = bits
        rest = rest - bf16_value(bits)
    forward = np.ascontiguousarray(table.reshape(TILES, P, SK).transpose(1, 0, 2))

    def even(b):
        return np.stack([b[0], 2 * b[1], 2 * b[2], b[3], b[4]])

    def odd(b):
        z = np.zeros_like(b[0])
        return np.stack([z, z, z, -b[4], b[3]])

    eh, ew, oh, ow = even(bh), even(bw), odd(bh), odd(bw)
    prod = lambda a, b: np.einsum("ih,jw->ijhw", a, b).reshape(NB, PIX) / PIX
    inverse = np.zeros((SK, RCH, 2, RC), np.float32)
    for part, g in enumerate((prod(eh, ew) - prod(oh, ow), prod(eh, ow) + prod(oh, ew))):
        hi = f32r(g)
        lo = f32r(g - hi)
        for block, v in enumerate((hi, lo, hi)):
            inverse[block * SBLK:block * SBLK + NB, :, part, :] = v.reshape(NB, RCH, RC)
    return forward, np.ascontiguousarray(inverse)


def small_constants():
    out = np.zeros((P, 2 * P + SK), np.float32)
    out[:, :P] = np.eye(P)
    out[:, P:2 * P] = np.kron(np.eye(P // GC), np.full((GC, GC), 1.0 / GC))
    for a in range(3):
        for b in range(3):
            for r in range(NB):
                out[a * SBLK + r, 2 * P + b * SBLK + r] = 1.0
    return out


def past(value):
    return not isinstance(value, int) or value > 0


def peeled(eng, count, body):
    body(0, True)
    with eng.Fori(1, count) as i:
        body(i, False)


def alternating(eng, body, lo, hi):
    if lo == 0:
        body(0, 0, 0)
        body(1, 1, 0)
    if hi > max(lo, 1):
        with eng.Fori(max(lo, 1), hi) as j:
            body(2 * j, 0, j)
            body(2 * j + 1, 1, j)


def build(nc, x, wqT, bq, wvT, bv, wconv, forward, inverse, consts, out):
    ctx = ExitStack()
    with ctx:
        def sb(name, shape, dt=F32):
            return ctx.enter_context(nc.sbuf_tensor(name, shape, dt))

        def sem(name):
            return ctx.enter_context(nc.semaphore(name))

        value = sb("value", [P, HALVES, PIX])
        rstd = sb("rstd", [P, 2, HALVES])
        nbias = sb("nbias", [P, 2, HALVES])
        zeros = sb("zeros", [P, HALVES, W])

        front = ExitStack()

        def fb(name, shape, dt=F32):
            return front.enter_context(nc.sbuf_tensor(name, shape, dt))

        with nc.sbuf_tensor("xn", [P, HALVES, PIX], F32) as xn:
            pass
        u_w = sb("u_w", [P, NK, POS, 2, C], F32R)
        region_w = fb("region_w", [P, NK * 3 * C])
        fwd_words = TILES * SK // 2
        fwd_u16 = region_w[:, 0:fwd_words].bitcast(U16)
        fwd_sb = region_w[:, 0:fwd_words].bitcast(BF16)
        raw = region_w[:, 0:NK * 3 * C].rearrange("p (n r o) -> p n r o", n=NK, r=3)
        bq_rows = region_w[:, fwd_words:fwd_words + C]
        bq_rest = region_w[:, fwd_words + C:fwd_words + 2 * C]
        sums_sb = region_w[:, fwd_words + 2 * C:fwd_words + 3 * C]
        scratch = fb("scratch", [P, 5632])
        level = scratch[:, 0:2048].rearrange("p (s a n) -> p s a n", s=2, a=HALVES)
        nearest = scratch[:, 2048:3072].bitcast(BF16).rearrange("p (s a n) -> p s a n", s=2, a=HALVES)
        whole = scratch[:, 3072:4096].bitcast(BF16).rearrange("p (s a n) -> p s a n", s=2, a=HALVES)
        qT = scratch[:, 4096:5120].bitcast(BF16).rearrange("p (s t c) -> p s t c", s=2, t=CT)
        wv_sb = scratch[:, 5120:5632].rearrange("p (a o) -> p a o", a=HALVES)
        table_ring = fb("table_ring", [SK, MEMBERS, 2, RC], F32R)
        sq_re = scratch[:, 0:HALVES * RC]
        sq_im = scratch[:, HALVES * RC:2 * HALVES * RC]
        fq = scratch[:, 2 * HALVES * RC:5 * HALVES * RC].rearrange("p (u a n) -> p u a n", u=MEMBERS, a=HALVES)
        x_ring = scratch[:, 5 * HALVES * RC:5 * HALVES * RC + 3 * RC].rearrange("p (u n) -> p u n", u=3)
        mask_rep = scratch[:, 5 * HALVES * RC + 3 * RC:5 * HALVES * RC + 4 * RC].rearrange(
            "p (d g k) -> p d g k", d=RT, k=MODS)
        w_sum = fb("w_sum", [P, 2, C])
        w_exact = fb("w_exact", [P, 4, C])
        class_max = fb("class_max", [P, MEMBERS, MODS, RT])
        column_max = fb("column_max", [P, MEMBERS * MODS, RT])
        wq_sb = fb("wq_sb", [P, HALVES, C])
        cst = fb("cst", [P, 2 * P + SK])
        ident, group_mean, stacker = cst[:, 0:P], cst[:, P:2 * P], cst[0:SK, 2 * P:2 * P + SK]
        ident_b = fb("ident_b", [P, P], BF16)
        ones_b = fb("ones_b", [SK, P], BF16)
        bq_parts = fb("bq_parts", [SK, C], BF16)
        bq_cast = fb("bq_cast", [SK, C], BF16)
        stacked = fb("stacked", [SK, C], F32R)
        bv_sb = fb("bv_sb", [P, HALVES])
        stats = fb("stats", [P, HALVES, RCH, 6])
        shift = fb("shift", [P, 1])
        sums_x = fb("sums_x", [P, 3, len(ACT_LOADS)])
        mv = fb("mv", [P, HALVES, 2])
        gn_t = fb("gn_t", [P, 8, HALVES])
        ext = fb("ext", [P, 2, LOADS])
        qz = fb("qz", [P, 6, HALVES])

        front.close()
        v_ring = sb("v_ring", [P, VS, 2, TR, HALVES, W + 2], F32R)
        xc = sb("xc", [P, XR, HALVES, W])
        t_buf = sb("t_buf", [P, 2, TR, HALVES * W])
        v_buf = sb("v_buf", [P, 2, TR, HALVES * W])
        odd_b = sb("odd_b", [P, HALVES, TR, W])
        sum_b = sb("sum_b", [P, HALVES, TR, W])

        psum = ctx.enter_context(nc.psum_tensor("psum", [P, 8, CHUNK], F32))
        qT_ps = psum[:, 0:2].rearrange("p s n -> p (s n)").bitcast(BF16).rearrange(
            "p (s t c) -> p s t c", s=2, t=CT)
        v_ps = psum[:, 4:6]
        v_first_ps = [psum[:, 2 * c:2 * c + 2] for c in range(LOADW // CHUNK)]
        sums_ps = psum[:, 6]
        small_ps = psum[:, 7]
        field_ps = psum[:, 0:4, 0:RC].rearrange("p (f a) n -> p f a n", f=2)
        query_ps = psum[:, 4:4 + RT, 0:C]
        mask_ps = psum[:, 7, 0:RC]

        s_x = [[sem(f"x_in{a}_{i}") for i in range(LOADS)] for a in range(HALVES)]
        s_cst, s_wv, s_bias, s_fwd, s_wq = (sem(n) for n in (
            "cst_in", "wv_in", "bias_in", "fwd_in", "wq_in"))
        s_table = [sem(f"table_in{u}") for u in range(MEMBERS)]
        s_xr = [sem(f"x_again{u}") for u in range(3)]
        dve_step = sem("dve_step")
        s_prep, s_bq = sem("prep_done"), sem("bq_parts_step")
        s_ident = sem("bf16_identities")
        s_gps = sem("group_psum")
        s_gin = sem("group_in")
        s_var = sem("variance_ready")
        s_std = sem("std_ready")
        s_norm = sem("norm_ready")
        s_shift, s_sums = sem("shift_ready"), sem("shifted_sums")
        s_xn = [sem("xn_ready0"), sem("xn_ready1")]
        s_ext = sem("extrema_ready")
        s_qz = sem("level_scale_ready")
        s_abs, s_level, s_near, s_above, s_quant = (sem(n) for n in (
            "abs_ready", "level_ready", "nearest_ready", "above_ready", "quantised"))
        s_T, s_qT, s_dft = sem("transposed"), sem("qT_ready"), sem("sums_added")
        s_v, s_vout = sem("v_product"), sem("v_ready")
        s_ssb, s_stack_ps, s_stack = (sem(n) for n in ("sums_copied", "sums_stacked_psum", "sums_stacked"))
        s_field, s_sq, s_pow, s_fq = (sem(n) for n in (
            "field_ready", "squares_ready", "power_ready", "fq_ready"))
        s_query, s_qmax = sem("query_ready"), sem("query_reduced")
        s_col, s_rep, s_mT = sem("column_max_step"), sem("mask_spread"), sem("mask_transposed")
        s_gain, s_x1, s_stat2 = sem("gained"), sem("x1_ready"), sem("x1_counted")
        s_raw = [sem("raw_in_first"), sem("raw_in_last")]
        s_wexact, s_whi, s_wlo = sem("weight_exact"), sem("weight_hi"), sem("weight_lo")
        s_zero, s_halo, s_xc = sem("zeros_ready"), sem("halo_ready"), sem("chunk_rows_ready")
        s_t, s_vt, s_hi, s_lo = (sem(n) for n in ("transform_step", "transformed", "hi_ready", "lo_ready"))
        s_m, s_e, s_sd, s_y = (sem(n) for n in ("product_ready", "product_copied", "sum_diff_ready", "rows_added"))
        s_stored = sem("out_stored")

        block = ctx.enter_context(nc.Block())

        def weight(n, p):
            if p < 4:
                return w_exact[:, p]
            return raw[:, bass.ds(n, 1), (0, 2)[p - 4]].rearrange("p o c -> p (o c)")

        def weight_part(n, p, part):
            return u_w[:, bass.ds(n, 1), p, part].rearrange("p o c -> p (o c)")

        def member(i, j):
            return bass.ds((i + TRIPLES * j) * RC, RC)

        def transformed(p):
            return v_buf[:, p % 2].rearrange("p t (k w) -> p (t k) w", w=W)

        def split_part(p, part):
            return v_ring[:, p % VS, part, :, :, 1:W + 1].rearrange("p t k w -> p (t k) w")

        def product(p, m):
            return psum[:, (HALVES * p + m) % 6, 0:TR * W].rearrange("p (t w) -> p t w", w=W)

        @block.sync
        def _(sp):
            for a in range(HALVES):
                for i in range(LOADS):
                    sp.dma_start(xn[:, a, i * LOADW:(i + 1) * LOADW],
                                 x[a * P:(a + 1) * P, i * LOADW:(i + 1) * LOADW]).then_inc(s_x[a][i], 16)
                if a == 0:
                    sp.dma_start(cst[:, :], consts).then_inc(s_cst, 16)
                    sp.dma_start(wv_sb, wvT.rearrange("(a p) o -> p a o", p=P)).then_inc(s_wv, 16)
            sp.dma_start(fwd_u16, forward.rearrange("p t k -> p (t k)")).then_inc(s_fwd, 16)
            sp.dma_start(wq_sb[:, :, :], wqT.rearrange("(a p) o -> p a o", p=P)).then_inc(s_wq, 16)
            sp.dma_start(bv_sb[:, :], bv).then_inc(s_bias, 16)
            sp.wait_ge(s_prep, 3)
            for r in range(3):
                sp.dma_start(bq_rows[r * SBLK:r * SBLK + 1, :], bq.rearrange("(a n) -> a n", a=1)
                             ).then_inc(s_bias, 16)

            for n in range(NK):
                used = -(-(n + 1) * 3 * C // (CT * SK // 2))
                if used > CHUNKS:
                    sp.wait_ge(s_bq, 8)
                    sp.wait_ge(s_stack_ps, 1)
                sp.wait_ge(s_dft, min(used, CHUNKS))
                sp.dma_start(raw[:, n], wconv.rearrange("(a p) (s r o) -> a p s r o", p=P, s=3, r=3)[n // 3, :, n % 3]
                             ).then_inc(s_raw[used > CHUNKS], 16)

            def x_again(i, first):
                for n in range(MEMBERS * HALVES):
                    j, a = n // HALVES, n % HALVES
                    if past(6 * i + n - 2):
                        sp.wait_ge(s_x1, 6 * i + n - 2)
                    sp.dma_start(x_ring[:, n % 3], x[a * P:(a + 1) * P, member(i, j)]).then_inc(s_xr[n % 3], 16)

            sp.wait_ge(s_v, 2 * CHUNKS)
            peeled(sp, TRIPLES, x_again)
            with sp.Fori(0, CCH) as i:
                sp.wait_ge(s_y, YS * i + YS)
                sp.dma_start(out.rearrange("(a p) n -> p a n", p=P)[:, :, bass.ds(i * CW, CW)],
                             value[:, :, bass.ds(i * CW, CW)]).then_inc(s_stored, 16)
            sp.wait_ge(s_stored, 16 * CCH)

        @block.gpsimd
        def _(pool):
            def table(i, j):
                pool.dma_start(table_ring[:, j], inverse[:, bass.ds(i + TRIPLES * j, 1)].rearrange(
                    "k o f n -> k (o f) n")).then_inc(s_table[j], 16)

            pool.memset(bq_rows[0:SK, :], 0.0).then_inc(s_prep, 1)
            pool.memset(ones_b[:, :], 1.0).then_inc(s_prep, 1)
            pool.memset(bq_parts[:, :], 0.0).then_inc(s_prep, 1)
            pool.memset(zeros[:, :, :], 0.0).then_inc(s_zero, 1)
            for j in range(MEMBERS):
                table(0, j)
            pool.wait_ge(s_norm, 1)
            for c in range(LOADS):
                v = xn[:, 0, c * LOADW:(c + 1) * LOADW]
                pool.tensor_scalar(v, v, rstd[:, 0, 0:1], nbias[:, 0, 0:1], ALU.mult, ALU.add).then_inc(s_xn[0], 1)

            def residual(i, j):
                for a in range(HALVES):
                    n = HALVES * j + a
                    pool.wait_ge(s_xr[n % 3], 16 * (2 * i + n // 3 + 1))
                    pool.wait_ge(s_gain, 6 * i + n + 1)
                    v = value[:, a, member(i, j)]
                    pool.tensor_tensor(v, v, x_ring[:, n % 3], ALU.add).then_inc(s_x1, 1)

            def weights_lo(n, j):
                for k, p in enumerate(((4, 5), (0, 1), (2, 3))[j]):
                    pool.wait_ge(s_whi, 6 * n + 2 * j + k + 1)
                    pool.tensor_tensor(weight_part(n, p, 1), weight(n, p), weight_part(n, p, 0).bitcast(F32),
                                       ALU.subtract).then_inc(s_wlo, 1)

            def triple(i, tables=True, before=True, unit=None):
                for j in range(MEMBERS):
                    if tables:
                        pool.wait_ge(s_field, 3 * i + j + 1)
                        table(i + 1, j)
                    if before:
                        residual(i - 1, j)
                    if unit is not None:
                        weights_lo(unit, j)

            pool.wait_ge(s_bias, 16 * 4)
            done = 0
            for part in range(3):
                rows = slice(part * SBLK, part * SBLK + 1)
                src = bq_rows if part == 0 else bq_rest
                pool.tensor_copy(bq_cast[:, :], src[0:SK, :]).then_inc(s_bq, 1)
                pool.wait_ge(s_bq, done + 1)
                pool.tensor_copy(bq_parts[rows, :], bq_cast[rows, :]).then_inc(s_bq, 1)
                pool.wait_ge(s_bq, done + 2)
                if part < 2:
                    pool.tensor_tensor(bq_rest[0:SK, :], src[0:SK, :], bq_cast[:, :], ALU.subtract).then_inc(s_bq, 1)
                    pool.wait_ge(s_bq, done + 3)
                done += 3
            triple(0, before=False, unit=0)
            with pool.Fori(1, NK) as i:
                triple(i, unit=i)
            with pool.Fori(NK, TRIPLES - 1) as i:
                triple(i)
            triple(TRIPLES - 1, tables=False)
            triple(TRIPLES, tables=False)
            pool.wait_ge(s_norm, 3)
            for col in (0, W + 1):
                pool.memset(v_ring[:, :, :, :, :, col:col + 1].rearrange("p s l t k c -> p (s l t k) c").bitcast(F32), 0.0
                            ).then_inc(s_zero, 1)

        @block.scalar
        def _(act):
            def std(n, lo, hi):
                act.wait_ge(s_var, n)
                act.activation(gn_t[:, 4, lo:hi], gn_t[:, 3, lo:hi], ACT.Sqrt).then_inc(s_std, 1)

            def normalise(i):
                v = xn[:, 1, i * LOADW:(i + 1) * LOADW]
                act.activation(v, v, ACT.Identity, bias=nbias[:, 0, 1:2], scale=rstd[:, 0, 1:2]).then_inc(s_xn[1], 1)

            def shifted_sums():
                act.wait_ge(s_shift, 1)
                for n, i in enumerate(ACT_LOADS):
                    act.wait_ge(s_x[1][i], 16)
                    for k, func in enumerate((ACT.Identity, ACT.Square)):
                        act.activation(value[:, k, n * LOADW:(n + 1) * LOADW], xn[:, 1, i * LOADW:(i + 1) * LOADW],
                                       func, bias=shift[:, :], accum_out=sums_x[:, k, n:n + 1]).then_inc(s_sums, 1)

            def absolute(c, slot):
                act.activation(level[:, slot], xn[:, :, bass.ds(c * CHUNK, CHUNK)], ACT.Abs).then_inc(s_abs, 1)

            def levels(c, slot, j, copy=True):
                if past(c - 1):
                    act.wait_ge(s_above, c - 1)
                if past(c - 1):
                    absolute(c, slot)
                act.wait_ge(s_abs, c + 1)
                for a in range(HALVES):
                    act.activation(level[:, slot, a], level[:, slot, a], ACT.Relu, bias=qz[:, 4, a:a + 1],
                                   scale=qz[:, 3, a:a + 1]).then_inc(s_level, 1)
                if copy:
                    v_copy(j + (VLEAD - 1), slot)

            def v_copy(c, m, banks=v_ps):
                act.wait_ge(s_v, 2 * c + m + 1)
                act.activation(value[:, m, bass.ds(c * CHUNK, CHUNK)], banks[:, m],
                               ACT.Identity, bias=bv_sb[:, m:m + 1]).then_inc(s_vout, 1)

            std(1, 0, 1)
            shifted_sums()
            std(2, 1, 2)
            act.wait_ge(s_norm, 2)
            act.wait_ge(s_bias, 16 * 4)
            act.wait_ge(s_sums, 2 * len(ACT_LOADS))
            for i in range(LOADS):
                normalise(i)
                if 1 <= i <= LOADW // CHUNK:
                    for m in range(HALVES):
                        v_copy(i - 1, m, v_first_ps[i - 1])
            with act.Fori(LOADW // CHUNK, VLEAD) as c:
                v_copy(c, 0)
                v_copy(c, 1)
            act.wait_ge(s_xn[0], LOADS)
            absolute(0, 0)
            absolute(1, 1)
            act.wait_ge(s_qz, 2)
            alternating(act, lambda c, slot, j: levels(c, slot, j, copy=False), 0, 1)
            alternating(act, levels, 1, PAIRS)
            v_copy(CHUNKS - 2, 0)
            v_copy(CHUNKS - 2, 1)

            def squares(i, j):
                n = 3 * i + j
                act.wait_ge(s_field, n + 1)
                if past(n):
                    act.wait_ge(s_pow, n)
                act.activation(sq_im.rearrange("p (a n) -> p a n", a=HALVES), field_ps[:, 1], ACT.Square
                               ).then_inc(s_sq, 1)
                if past(n):
                    act.wait_ge(s_fq, n)
                act.activation(sq_re.rearrange("p (a n) -> p a n", a=HALVES), field_ps[:, 0], ACT.Square
                               ).then_inc(s_sq, 1)

            def root(i, j):
                n = 3 * i + j
                act.wait_ge(s_pow, n + 1)
                if past(3 * n - 6):
                    act.wait_ge(s_query, 3 * n - 6)
                act.activation(fq[:, j].rearrange("p a n -> p (a n)"), sq_re, ACT.Sqrt).then_inc(s_fq, 1)

            def spread(i, j):
                act.wait_ge(s_col, 5 * i + 5)
                if past(3 * i + j):
                    act.wait_ge(s_mT, 3 * i + j)
                src = column_max.rearrange("p (k j) (d g) -> p j d g k", j=MEMBERS, g=1)[:, j]
                act.activation(mask_rep, src.broadcast_to([P, RT, P // MODS, MODS]), ACT.Copy).then_inc(s_rep, 1)

            def weights_hi(n, j):
                if j > 0:
                    act.wait_ge(s_wexact, 6 * n + 2 * j + 2)
                for p in ((4, 5), (0, 1), (2, 3))[j]:
                    act.activation(weight_part(n, p, 0), weight(n, p), ACT.Copy).then_inc(s_whi, 1)

            def triple(i, query=True, before=True, unit=None):
                for j in range(MEMBERS):
                    if query:
                        squares(i, j)
                    if before and j > 0:
                        spread(i - 1, j - 1)
                    elif before and past(i - 1):
                        spread(i - 2, MEMBERS - 1)
                    if isinstance(i, int) and i == 0 and j == 0:
                        v_copy(CHUNKS - 1, 0)
                        v_copy(CHUNKS - 1, 1)
                    if query:
                        root(i, j)
                    if unit is not None:
                        weights_hi(unit, j)

            act.wait_ge(s_raw[0], 4 * 16)
            triple(0, before=False, unit=0)
            triple(1, unit=1)
            act.wait_ge(s_raw[1], 2 * 16)
            with act.Fori(2, NK) as i:
                triple(i, unit=i)
            with act.Fori(NK, TRIPLES) as i:
                triple(i)
            triple(TRIPLES, query=False)
            spread(TRIPLES - 1, MEMBERS - 1)
            std(3, 0, 2)
            act.wait_ge(s_norm, 3)
            act.wait_ge(s_zero, 3)

            def rows(c, lo, n, halves=(0, 1)):
                for k in halves:
                    src = value[:, k, bass.ds(c * CW + (lo - 1) * W, n * W)]
                    act.activation(xc[:, lo:lo + n, k, :], src.rearrange("p (h w) -> p h w", w=W), ACT.Identity,
                                   bias=nbias[:, 1, k:k + 1], scale=rstd[:, 1, k:k + 1]).then_inc(s_xc, 1)

            def next_rows(c, last=False):
                act.wait_ge(s_vt, POS * c)
                act.activation(xc[:, 0:2], xc[:, CR:XR], ACT.Copy).then_inc(s_halo, 1)
                act.wait_ge(s_halo, c + 1)
                if last:
                    act.activation(xc[:, XR - 1], zeros[:, :, :], ACT.Copy).then_inc(s_halo, 1)
                rows(c, 2, CR - 1 if last else CR)

            def hi(c, p, first=False):
                q = POS * c + p
                act.wait_ge(s_vt, q + 1)
                if not (first and p < VS):
                    act.wait_ge(s_m, 2 * q - 2 * VS + 2)
                act.activation(split_part(p, 0), transformed(p), ACT.Copy).then_inc(s_hi, 1)

            def copy_product(i, p, first):
                for m in range(HALVES):
                    act.wait_ge(s_m, 2 * (POS * i + p) + m + 1)
                    if p == 3 or not first:
                        act.wait_ge(s_y, YS * i + (8 if p == 3 else 0))
                    act.activation(odd_b[:, m], product(p, m), ACT.Copy).then_inc(s_e, 1)

            def conv_copies(i, first=False, before_last=False, last=False):
                for p in range(POS):
                    if p in (2, 4):
                        copy_product(i, p - 1, first)
                    if p < POS - 2:
                        hi(i, p + 2, first)
                    elif not last:
                        hi(i + 1, p + 2 - POS)
                    if p == 2 and not last:
                        next_rows(i + 1, before_last)

            act.activation(xc[:, 0], zeros[:, :, :], ACT.Copy).then_inc(s_halo, 1)
            rows(0, 1, XR - 1, (0,))
            hi(0, 0, True)
            hi(0, 1, True)
            conv_copies(0, first=True)
            with act.Fori(1, CCH - 2) as i:
                conv_copies(i)
            conv_copies(CCH - 2, before_last=True)
            conv_copies(CCH - 1, last=True)

        @block.tensor
        def _(pe):
            def group_sums(n, lo, hi):
                pe.wait_ge(s_gin, 2 * n + 1)
                pe.matmul(small_ps[:, 8 * n:8 * n + hi - lo], group_mean, mv[:, lo:hi, 0],
                          start=True, stop=True).then_inc(s_gps, 1)
                pe.wait_ge(s_gin, 2 * n + 2)
                pe.matmul(small_ps[:, 8 * n + 4:8 * n + 4 + hi - lo], group_mean, gn_t[:, 2, lo:hi],
                          start=True, stop=True).then_inc(s_gps, 1)

            def transposes(c, slot, j, v=True):
                if not past(c - 1):
                    v_half(j + VLEAD, slot)
                pe.wait_ge(s_quant, c + 1)
                if past(c - 1):
                    pe.wait_ge(s_qT, c - 1)
                for t in range(CT):
                    for a in range(HALVES):
                        last = pe.transpose(qT_ps[:, slot, t, a * P:(a + 1) * P],
                                            whole[:, slot, a, t * P:(t + 1) * P], ident_b[:, :])
                last.then_inc(s_T, 1)
                if v and past(c - 1):
                    v_half(j + VLEAD, slot)
                if past(c):
                    sums(c - 1, 1 - slot, start=isinstance(c, int) and c == 1)

            def sums(c, slot, start=False, stop=False):
                pe.wait_ge(s_qT, c + 1)
                for t in range(CT):
                    last = pe.matmul(sums_ps[0:SK, 0:C], fwd_sb[:, bass.ds((c * CT + t) * SK, SK)],
                                     qT[:, slot, t], start=start and t == 0, stop=stop and t == CT - 1)
                last.then_inc(s_dft, 1)

            def v_half(c, m):
                pe.wait_ge(s_vout, 2 * c + m - 1)
                for k in range(HALVES):
                    last = pe.matmul(v_ps[:, m], wv_sb[:, k, m * P:(m + 1) * P],
                                     xn[:, k, bass.ds(c * CHUNK, CHUNK)], start=k == 0, stop=k == HALVES - 1)
                last.then_inc(s_v, 1)

            pe.wait_ge(s_cst, 16)
            group_sums(0, 0, 1)

            def v_term(c, m, k):
                return pe.matmul(v_first_ps[c][:, m], wv_sb[:, k, m * P:(m + 1) * P],
                                 xn[:, k, c * CHUNK:(c + 1) * CHUNK], start=k == 0, stop=k == HALVES - 1)

            pe.wait_ge(s_wv, 16)
            pe.wait_ge(s_xn[0], 1)
            for c in range(LOADW // CHUNK):
                for m in range(HALVES):
                    v_term(c, m, 0)
            group_sums(1, 1, 2)
            pe.wait_ge(s_xn[1], 1)
            for c in range(LOADW // CHUNK):
                for m in range(HALVES):
                    v_term(c, m, 1).then_inc(s_v, 1)
            pe.wait_ge(s_xn[0], LOADS)
            pe.wait_ge(s_xn[1], -(-VLEAD * CHUNK // LOADW))
            with pe.Fori(LOADW // CHUNK, VLEAD) as c:
                v_half(c, 0)
                v_half(c, 1)
            pe.wait_ge(s_xn[1], LOADS)
            pe.wait_ge(s_ident, 1)
            pe.wait_ge(s_fwd, 16)
            alternating(pe, transposes, 0, PAIRS - 1)
            transposes(CHUNKS - 2, 0, PAIRS - 1)
            transposes(CHUNKS - 1, 1, PAIRS - 1, v=False)
            sums(CHUNKS - 1, 1, stop=True)
            pe.wait_ge(s_ssb, 1)
            pe.matmul(small_ps[0:SK, 0:C], stacker, sums_sb[0:SK, :], start=True, stop=True).then_inc(s_stack_ps, 1)

            def fields(i, j):
                n = 3 * i + j
                pe.wait_ge(s_table[j], 16 * (i + 1))
                for part in (1, 0):
                    if past(2 * n - part):
                        pe.wait_ge(s_sq, 2 * n - part)
                    for a in range(HALVES):
                        last = pe.matmul(field_ps[:, part, a], stacked[:, a * P:(a + 1) * P],
                                         table_ring[:, j, part], start=True, stop=True)
                last.then_inc(s_field, 1)

            def query(i, j):
                n = 3 * i + j
                pe.wait_ge(s_fq, n + 1)
                for d in range(RT):
                    if past(3 * n + d - 2):
                        pe.wait_ge(s_qmax, 3 * n + d - 2)
                    for a in range(HALVES):
                        pe.matmul(query_ps[:, d], fq[:, j, a, d * P:(d + 1) * P], wq_sb[:, a, :],
                                  start=a == 0, stop=False)
                    pe.matmul(query_ps[:, d], ones_b[:, :], bq_parts[:, :], start=False, stop=True
                              ).then_inc(s_query, 1)

            def mask_transposes(i, j):
                pe.wait_ge(s_rep, 3 * i + j + 1)
                if past(6 * i + 2 * j):
                    pe.wait_ge(s_gain, 6 * i + 2 * j)
                for d in range(RT):
                    last = pe.transpose(mask_ps[:, d * P:(d + 1) * P],
                                        mask_rep[:, d].rearrange("p g k -> p (g k)"), ident)
                last.then_inc(s_mT, 1)

            def triple(i, last=False, before=True):
                for j in range(MEMBERS):
                    if j < MEMBERS - 1:
                        fields(i, j + 1)
                    elif not last:
                        fields(i + 1, 0)
                    if isinstance(i, int) and i == 0 and j == 0:
                        pe.wait_ge(s_vout, 2 * CHUNKS)
                    query(i, j)
                    if before:
                        mask_transposes(i - 1, j)

            v_half(CHUNKS - 2, 1)
            pe.wait_ge(s_stack, 1)
            fields(0, 0)
            v_half(CHUNKS - 1, 0)
            v_half(CHUNKS - 1, 1)
            pe.wait_ge(s_wq, 16)
            pe.wait_ge(s_bq, 8)
            triple(0, before=False)
            triple(1)
            with pe.Fori(2, TRIPLES - 1) as i:
                triple(i)
            triple(TRIPLES - 1, last=True)
            for j in range(MEMBERS):
                mask_transposes(TRIPLES - 1, j)
            group_sums(2, 0, 2)

            def conv(i, first):
                for p in range(POS):
                    pe.wait_ge(s_lo, POS * i + p + 1)
                    for m in range(HALVES):
                        if p in (3, 5):
                            pe.wait_ge(s_sd, 8 * i + (3 if p == 3 else 7) + m)
                        elif p == 4:
                            pe.wait_ge(s_e, 4 * i + m + 1)
                        elif p == 0 and not first:
                            pe.wait_ge(s_e, 4 * i - 1 + m)
                        elif not first:
                            pe.wait_ge(s_y, YS * i - (3 if p == 1 else 1) + m)
                        for n in range(NK):
                            for j, (wl, vl) in enumerate(((0, 0), (0, 1), (1, 0))):
                                last = pe.matmul(product(p, m).rearrange("p t w -> p (t w)"),
                                                 u_w[:, n, p, wl, m * P:(m + 1) * P],
                                                 v_ring[:, p % VS, vl, :, n // 3, n % 3:n % 3 + W],
                                                 start=n == 0 and j == 0, stop=n == NK - 1 and j == 2)
                        last.then_inc(s_m, 1)

            pe.wait_ge(s_wlo, POS * NK)
            peeled(pe, CCH, conv)

        @block.vector
        def _(dve):
            steps = [0]

            def mark(ins):
                steps[0] += 1
                ins.then_inc(dve_step, 1)

            def step(ins):
                mark(ins)
                dve.wait_ge(dve_step, steps[0])

            def group_norm(layer, n, lo, hi, parts=CHUNKS):
                w = hi - lo
                row = [gn_t[:, j, lo:hi] for j in range(8)]
                for a in range(lo, hi):
                    ins = dve.bn_aggr(mv[:, a, :], stats[:, a, 0:parts].rearrange("p c s -> p (c s)"))
                ins.then_inc(s_gin, 1)
                dve.wait_ge(s_gin, 2 * n + 1)
                dve.wait_ge(s_gps, 2 * n + 1)
                mean = small_ps[:, 8 * n:8 * n + w]
                mark(dve.tensor_tensor(row[0], mv[:, lo:hi, 0], mean, ALU.subtract))
                step(dve.tensor_copy(row[1], mean))
                step(dve.tensor_tensor(row[2], row[0], row[0], ALU.mult))
                dve.tensor_tensor(row[2], row[2], mv[:, lo:hi, 1], ALU.add).then_inc(s_gin, 1)
                dve.wait_ge(s_gps, 2 * n + 2)
                dve.tensor_scalar(row[3], small_ps[:, 8 * n + 4:8 * n + 4 + w], EPS, None, ALU.add
                                  ).then_inc(s_var, 1)
                dve.wait_ge(s_std, n + 1)
                dve.wait_ge(s_var, n + 1)
                step(dve.reciprocal(row[5], row[4]))
                step(dve.tensor_tensor(row[6], row[5], row[5], ALU.mult))
                step(dve.tensor_tensor(row[6], row[6], row[3], ALU.mult))
                step(dve.tensor_scalar(row[6], row[6], -0.5, 1.5, ALU.mult, ALU.add))
                step(dve.tensor_tensor(rstd[:, layer, lo:hi], row[5], row[6], ALU.mult))
                dve.scalar_tensor_tensor(nbias[:, layer, lo:hi], row[1], -1.0, rstd[:, layer, lo:hi],
                                         ALU.mult, ALU.mult).then_inc(s_norm, 1)

            def load_stats(a, i, at):
                dve.wait_ge(s_x[a][i], 16)
                for j in range(LOADW // CHUNK):
                    ins = dve.bn_stats(stats[:, a, at + j],
                                       xn[:, a, i * LOADW + j * CHUNK:i * LOADW + (j + 1) * CHUNK])
                return ins

            tuples = stats[:, 1].rearrange("p c (h s) -> p (c h) s", s=3)
            act_at = 4 * (LOADW // CHUNK)
            act_tuples = tuples[:, act_at:act_at + len(ACT_LOADS)]

            def act_stats():
                dve.wait_ge(s_sums, 2 * len(ACT_LOADS))
                step(dve.tensor_scalar(sums_x[:, 2], sums_x[:, 0], 1.0 / LOADW, None, ALU.mult))
                mark(dve.tensor_scalar(act_tuples[:, :, 1], sums_x[:, 2], shift[:, :], None, ALU.subtract))
                step(dve.scalar_tensor_tensor(sums_x[:, 2], sums_x[:, 2], -1.0, sums_x[:, 0], ALU.mult, ALU.mult))
                step(dve.tensor_tensor(act_tuples[:, :, 2], sums_x[:, 1], sums_x[:, 2], ALU.add))

            def extrema_of(a, c):
                dve.wait_ge(s_xn[a], c + 1)
                for j, op in enumerate((ALU.max, ALU.min)):
                    dve.tensor_reduce(ext[:, j, bass.ds(c, 1)], xn[:, a, bass.ds(c * LOADW, LOADW)], AX.X, op,
                                      apply_absolute_value=True).then_inc(s_ext, 1)

            def level_scale(a):
                dve.wait_ge(s_ext, 2 * LOADS * (a + 1))
                z = [qz[:, j, a:a + 1] for j in range(6)]
                step(dve.tensor_reduce(z[0], ext[:, 0, 0:LOADS], AX.X, ALU.max))
                step(dve.tensor_reduce(z[1], ext[:, 1, 0:LOADS], AX.X, ALU.min))
                step(dve.tensor_tensor(z[2], z[0], z[1], ALU.subtract))
                step(dve.reciprocal(z[5], z[2]))
                step(dve.tensor_scalar(z[3], z[5], 255.0 * (1.0 + 2.0 ** -22), None, ALU.mult))
                dve.scalar_tensor_tensor(z[4], z[1], -1.0, z[3], ALU.mult, ALU.mult).then_inc(s_qz, 1)

            def flat(t):
                return t.rearrange("p a n -> p (a n)")

            def quantise(c, slot, j):
                dve.wait_ge(s_level, 2 * c + 2)
                if past(c - 1):
                    dve.wait_ge(s_T, c - 1)
                near, out_ = flat(nearest[:, slot]), flat(whole[:, slot])
                dve.tensor_scalar(near, flat(level[:, slot]), ROUND, -ROUND, ALU.add, ALU.add).then_inc(s_near, 1)
                dve.wait_ge(s_near, c + 1)
                dve.tensor_tensor(out_, flat(level[:, slot]), near, ALU.is_lt).then_inc(s_above, 1)
                if past(c):
                    copy_tiles(c - 1, 1 - slot)
                dve.wait_ge(s_above, c + 1)
                dve.tensor_tensor(out_, near, out_, ALU.subtract).then_inc(s_quant, 1)

            def copy_tiles(c, slot):
                dve.wait_ge(s_T, c + 1)
                if past(c - 1):
                    dve.wait_ge(s_dft, c - 1)
                dve.tensor_copy(qT[:, slot], qT_ps[:, slot]).then_inc(s_qT, 1)

            mark(dve.memset(act_tuples[:, :, 0], float(LOADW)))
            for i in range(LOADS):
                ins = load_stats(0, i, i * (LOADW // CHUNK))
            step(ins)
            group_norm(0, 0, 0, 1)
            step(load_stats(1, 0, 0))
            dve.tensor_scalar(shift[:, :], stats[:, 1, 0, 1:2], -1.0, None, ALU.mult).then_inc(s_shift, 1)
            dve.tensor_copy(ident_b[:, :], ident).then_inc(s_ident, 1)
            dve.wait_ge(s_shift, 1)
            with dve.Fori(0, EXT_FIRST) as c:
                extrema_of(0, c)
            step(load_stats(1, LOADS - 1, LOADW // CHUNK))
            act_stats()
            group_norm(0, 1, 1, 2, 2 * (LOADW // CHUNK) + len(ACT_LOADS) // 2)
            with dve.Fori(EXT_FIRST, LOADS) as c:
                extrema_of(0, c)
            level_scale(0)
            with dve.Fori(0, LOADS) as c:
                extrema_of(1, c)
            level_scale(1)
            alternating(dve, quantise, 0, PAIRS)
            copy_tiles(CHUNKS - 1, 1)

            dve.wait_ge(s_dft, CHUNKS)
            dve.tensor_copy(sums_sb[0:SK, :], sums_ps[0:SK, 0:C]).then_inc(s_ssb, 1)
            dve.wait_ge(s_stack_ps, 1)
            step(dve.tensor_copy(stacked[:, :], small_ps[0:SK, 0:C]))
            lo = slice(2 * SBLK, SK)
            dve.tensor_tensor(stacked[lo, :], small_ps[lo, 0:C], stacked[lo, :].bitcast(F32), ALU.subtract
                              ).then_inc(s_stack, 1)

            def power(c):
                dve.wait_ge(s_sq, 2 * c + 2)
                dve.tensor_tensor(sq_re, sq_re, sq_im, ALU.add).then_inc(s_pow, 1)

            def weights(n, part):
                g = [raw[:, bass.ds(n, 1), k].rearrange("p o c -> p (o c)") for k in range(3)]
                a, b = w_sum[:, 0], w_sum[:, 1]
                if part == 0:
                    if past(n):
                        dve.wait_ge(s_wexact, 6 * n)
                    dve.tensor_tensor(a, g[0], g[2], ALU.add).then_inc(s_wexact, 1)
                    dve.scalar_tensor_tensor(b, g[2], 4.0, g[0], ALU.mult, ALU.add).then_inc(s_wexact, 1)
                    return
                if part == 1:
                    dve.wait_ge(s_wexact, 6 * n + 2)
                    if past(n):
                        dve.wait_ge(s_wlo, 6 * n - 2)
                    dve.tensor_tensor(w_exact[:, 0], a, g[1], ALU.add).then_inc(s_wexact, 1)
                    dve.tensor_tensor(w_exact[:, 1], a, g[1], ALU.subtract).then_inc(s_wexact, 1)
                else:
                    if past(n):
                        dve.wait_ge(s_wlo, 6 * n)
                    for p, factor in ((2, 2.0), (3, -2.0)):
                        dve.scalar_tensor_tensor(w_exact[:, p], g[1], factor, b, ALU.mult, ALU.add
                                                 ).then_inc(s_wexact, 1)

            def query_max(i, j):
                n = 3 * i + j
                if past(5 * i):
                    dve.wait_ge(s_col, 5 * i)
                for d in range(RT):
                    dve.wait_ge(s_query, 3 * n + d + 1)
                    dve.tensor_reduce(class_max[:, j, :, d], query_ps[:, d].rearrange("p (c k) -> p k c", k=MODS),
                                      AX.X, ALU.max).then_inc(s_qmax, 1)

            def columns_of_two(i):
                dve.wait_ge(s_qmax, 9 * i + 9)
                if past(3 * i):
                    dve.wait_ge(s_rep, 3 * i)
                for lo, hi, src in ((1, MODS, slice(0, MODS - 1)), (0, 1, slice(MODS - 1, MODS))):
                    dve.tensor_tensor(column_max[:, lo:hi], class_max[:, 0, lo:hi], class_max[:, 1, src], ALU.max
                                      ).then_inc(s_col, 1)

            def columns_of_three(i):
                dve.wait_ge(s_col, 5 * i + 2)
                for lo, hi, src in ((2, MODS, slice(0, MODS - 2)), (0, 2, slice(MODS - 2, MODS))):
                    dve.tensor_tensor(column_max[:, lo:hi], column_max[:, lo:hi], class_max[:, 2, src], ALU.max
                                      ).then_inc(s_col, 1)

            def columns_again(i):
                dve.wait_ge(s_col, 5 * i + 4)
                copies = column_max[:, MODS:].rearrange("p (b s) d -> p b (s d)", b=MEMBERS - 1)
                dve.tensor_copy(copies, column_max[:, 0:MODS].rearrange("p (b s) d -> p b (s d)", b=1).broadcast_to(
                    [P, MEMBERS - 1, MODS * RT])).then_inc(s_col, 1)

            def gain(i, j, a):
                v = value[:, a, member(i, j)]
                dve.scalar_tensor_tensor(v, mask_ps, 1.0, v, ALU.add, ALU.mult).then_inc(s_gain, 1)

            def x1_stats(i, j):
                for a in range(HALVES):
                    dve.wait_ge(s_x1, 6 * i + 2 * j + a + 1)
                    dve.bn_stats(stats[:, a, bass.ds(i + TRIPLES * j, 1)].rearrange("p o s -> p (o s)"),
                                 value[:, a, member(i, j)]).then_inc(s_stat2, 1)

            def triple(i, query=True, last=False, before=True, unit=None, next_unit=None):
                for j in range(MEMBERS):
                    maxima = query and j == MEMBERS - 1
                    if query and not (last and maxima):
                        power(3 * i + j + 1)
                    if query:
                        query_max(i, j)
                    if before:
                        dve.wait_ge(s_mT, 3 * (i - 1) + j + 1)
                        gain(i - 1, j, 0)
                    if maxima:
                        columns_of_two(i)
                    if before:
                        gain(i - 1, j, 1)
                    if maxima:
                        columns_of_three(i)
                    if j == 0 and unit is not None:
                        weights(unit, 2)
                    elif maxima and next_unit is not None:
                        weights(next_unit, 0)
                    if maxima:
                        columns_again(i)
                    if maxima and next_unit is not None:
                        weights(next_unit, 1)
                    if before and j > 0:
                        x1_stats(i - 1, j - 1)
                    elif before and past(i - 1):
                        x1_stats(i - 2, MEMBERS - 1)

            power(0)
            dve.wait_ge(s_raw[0], 4 * 16)
            weights(0, 0)
            weights(0, 1)
            triple(0, before=False, unit=0, next_unit=1)
            triple(1, unit=1, next_unit=2)
            dve.wait_ge(s_raw[1], 2 * 16)
            with dve.Fori(2, NK - 1) as i:
                triple(i, unit=i, next_unit=i + 1)
            triple(NK - 1, unit=NK - 1)
            with dve.Fori(NK, TRIPLES - 1) as i:
                triple(i)
            triple(TRIPLES - 1, last=True)
            triple(TRIPLES, query=False)
            x1_stats(TRIPLES - 1, MEMBERS - 1)
            dve.wait_ge(s_stat2, 2 * RCH)
            group_norm(1, 2, 0, 2, RCH)

            def transform(c, p):
                d = [xc[:, j:j + WT * (TR - 1) + 1:WT].rearrange("p t k w -> p t (k w)") for j in range(6)]
                v, t1, t2 = v_buf[:, p % 2], t_buf[:, 0], t_buf[:, 1]
                steps = (2, 2, 4, 4, 5, 6)[p]
                first = isinstance(c, int) and c == 0
                if p == 0:
                    dve.wait_ge(s_xc, 2 * c + 1)
                if p in (0, 2, 4, 5) and not (first and p == 0):
                    dve.wait_ge(s_vt, POS * c + p)
                if p == 0:
                    dve.scalar_tensor_tensor(t1, d[2], -4.0, d[4], ALU.mult, ALU.add).then_inc(s_t, 1)
                    dve.scalar_tensor_tensor(t2, d[1], -4.0, d[3], ALU.mult, ALU.add).then_inc(s_t, 1)
                elif p == 2:
                    dve.tensor_tensor(t1, d[4], d[2], ALU.subtract).then_inc(s_t, 1)
                    dve.tensor_tensor(t2, d[3], d[1], ALU.subtract).then_inc(s_t, 1)
                elif p == 4:
                    dve.scalar_tensor_tensor(t1, d[2], -5.0, d[4], ALU.mult, ALU.add).then_inc(s_t, 1)
                elif p == 5:
                    dve.scalar_tensor_tensor(t2, d[3], -5.0, d[5], ALU.mult, ALU.add).then_inc(s_t, 1)
                dve.wait_ge(s_t, POS * c + steps)
                if not (first and p < 2):
                    dve.wait_ge(s_lo, POS * c + p - 1)
                if p == 0:
                    ins = dve.tensor_tensor(v, t1, t2, ALU.add)
                elif p == 1:
                    ins = dve.tensor_tensor(v, t1, t2, ALU.subtract)
                elif p in (2, 3):
                    ins = dve.scalar_tensor_tensor(v, t2, 2.0 if p == 2 else -2.0, t1, ALU.mult, ALU.add)
                else:
                    ins = dve.scalar_tensor_tensor(v, d[p - 4], 4.0, t1 if p == 4 else t2, ALU.mult, ALU.add)
                ins.then_inc(s_vt, 1)

            def split(c, p):
                dve.wait_ge(s_hi, POS * c + p + 1)
                dve.tensor_tensor(split_part(p, 1), transformed(p), split_part(p, 0).bitcast(F32), ALU.subtract
                                  ).then_inc(s_lo, 1)

            def out_rows(i, m, j, n=1):
                v = value[:, m, bass.ds(i * CW, CW)].rearrange("p (t j w) -> p j t w", j=WT, w=W)
                return v[:, j:j + 2 * n - 1:2]

            def add(i, m, j, term, factor):
                dst = out_rows(i, m, j).rearrange("p j t w -> p (j t) w")
                dve.scalar_tensor_tensor(dst, term, factor, dst, ALU.mult, ALU.add).then_inc(s_y, 1)

            def take(i, p, first=False):
                if p in (1, 3):
                    base = 8 * i + (0 if p == 1 else 4)
                    for m in range(HALVES):
                        dve.wait_ge(s_e, 4 * i + (p - 1) + m + 1)
                        if not (first and p == 1):
                            dve.wait_ge(s_y, YS * i + (0 if p == 1 else 8))
                        dve.tensor_tensor(sum_b[:, m], product(p - 1, m), odd_b[:, m], ALU.add
                                          ).then_inc(s_sd, 1)
                    for m in range(HALVES):
                        dve.wait_ge(s_sd, base + m + 1)
                        dve.tensor_tensor(odd_b[:, m], product(p - 1, m), odd_b[:, m], ALU.subtract
                                          ).then_inc(s_sd, 1)
                if p == 1:
                    for m in range(HALVES):
                        dve.wait_ge(s_sd, base + m + 3)
                        for j, term in ((0, sum_b), (1, odd_b)):
                            for jj in (j, j + 2):
                                add(i, m, jj, term[:, m], -1.0 / 6.0)
                elif p == 3:
                    for m in range(HALVES):
                        dve.wait_ge(s_sd, base + m + 3)
                        add(i, m, 0, sum_b[:, m], 1.0 / 24.0)
                        add(i, m, 2, sum_b[:, m], 4.0 / 24.0)
                        add(i, m, 1, odd_b[:, m], 2.0 / 24.0)
                        add(i, m, 3, odd_b[:, m], 8.0 / 24.0)
                elif p in (4, 5):
                    for m in range(HALVES):
                        dve.wait_ge(s_m, 2 * (POS * i + p) + m + 1)
                        dve.wait_ge(s_y, YS * i + 16)
                        add(i, m, 0 if p == 4 else 3, product(p, m), 0.25 if p == 4 else 1.0)

            def conv_steps(i, first=False, last=False):
                for p in range(POS):
                    if p < 3:
                        transform(i, p + 3)
                    elif not last:
                        transform(i + 1, p - 3)
                    if p == 0:
                        if not first:
                            take(i - 1, POS - 1)
                    else:
                        take(i, p - 1, first)
                    if p < POS - 2:
                        split(i, p + 2)
                    elif not last:
                        split(i + 1, p + 2 - POS)

            src = value[:, 1, 0:(XR - 1) * W]
            dve.wait_ge(s_norm, 3)
            step(dve.tensor_scalar(xc[:, 1:XR, 1, :], src.rearrange("p (h w) -> p h w", w=W), rstd[:, 1, 1:2],
                                   nbias[:, 1, 1:2], ALU.mult, ALU.add))
            transform(0, 0)
            transform(0, 1)
            split(0, 0)
            transform(0, 2)
            split(0, 1)
            conv_steps(0, first=True)
            with dve.Fori(1, CCH - 1) as i:
                conv_steps(i)
            conv_steps(CCH - 1, last=True)
            take(CCH - 1, POS - 1)


def kernel(x, L0_conv_Wq, L0_conv_bq, L0_conv_Wk, L0_conv_bk, L0_conv_Wv, L0_conv_bv, L1_conv_weight_matrix):
    import concourse.bacc as bacc
    from concourse.bass_utils import run_bass_kernel_spmd

    forward, inverse = frequency_tables()
    order = np.array([MODS * (n // MODS) + 3 * n % MODS for n in range(C)])
    arrays = {
        "x": np.ascontiguousarray(np.asarray(x).reshape(C, PIX)),
        "wqT": np.ascontiguousarray(np.asarray(L0_conv_Wq).T[:, order]),
        "bq": np.ascontiguousarray(np.asarray(L0_conv_bq)[order]),
        "wvT": np.ascontiguousarray(np.asarray(L0_conv_Wv).T),
        "bv": np.ascontiguousarray(np.asarray(L0_conv_bv).reshape(HALVES, P).T),
        "wconv": np.ascontiguousarray(
            np.asarray(L1_conv_weight_matrix).reshape(C, 3, 3, C).transpose(0, 2, 1, 3).reshape(C, 9 * C)),
        "forward": forward,
        "inverse": inverse,
        "consts": small_constants(),
    }
    nc = bacc.Bacc("TRN2", target_bir_lowering=False, num_devices=1)
    aps = {n: nc.dram_tensor(n, a.shape, mybir.dt.from_np(a.dtype), kind="ExternalInput").ap()
           for n, a in arrays.items()}
    out = nc.dram_tensor("out", (C, PIX), F32, kind="ExternalOutput").ap()
    build(nc, **aps, out=out)
    got = run_bass_kernel_spmd(nc, [arrays], core_ids=[0])
    return got.results[0]["out"].reshape(1, C, H, W)
```
